# Optimizing a Trainium2 kernel written in Bass

```python
import numpy as np
import jax
import jax.numpy as jnp

def _softmax(x, axis=-1):
    return jax.nn.softmax(x, axis=axis)

def _gelu(x):
    return jax.nn.gelu(x, approximate=True)

def _silu(x):
    return jax.nn.silu(x)

def _sigmoid(x):
    return jax.nn.sigmoid(x)

def _layernorm(x, axis=-1, eps=1e-05):
    m = jnp.mean(x, axis=axis, keepdims=True)
    v = jnp.var(x, axis=axis, keepdims=True)
    return (x - m) / jnp.sqrt(v + eps)

def _scatter_add(tgt, idx, src, axis=0):
    return tgt.at[idx].add(src)

def _segment_sum(src, seg, n):
    return jax.ops.segment_sum(src, seg, n)
kernel_name = 'mk_adj_ffn_d2_adj_r2_f52f26'

def setup_inputs(seed: int=0):
    np.random.seed(seed)
    _w = jnp.asarray

    def _rec_inputs():
        import jax
        import jax.numpy as jnp
        _gk = jax.random.key(seed)
        x = 7.22e-05 + 1 * jax.random.normal(jax.random.fold_in(_gk, 1), (64, 128, 128), jnp.float32)
        _a = jax.random.bernoulli(jax.random.fold_in(_gk, 2), 0.015625, (64, 128, 128))
        _a = jnp.logical_or(_a, jnp.eye(128, dtype=bool))
        _af = _a.astype(jnp.float32)
        _af = _af * jax.random.uniform(jax.random.fold_in(_gk, 3), (64, 128, 128), jnp.float32, 0.05, 1)
        adj = _af
        return (x, adj)
    x, adj = _rec_inputs()

    def _L0_gnn_setup():
        import jax, jax.numpy as jnp
        import numpy as np
        D_IN = 128
        D_HID = 256
        key = jax.random.key(seed)
        k1, k2, k3, k4, k5, k6 = jax.random.split(key, 6)
        x = jax.random.normal(k1, (8, 2048, D_IN), dtype=jnp.float32)
        adj = jax.random.uniform(k2, (8, 2048, 2048), dtype=jnp.float32)
        s1 = 1.0 / np.sqrt(D_IN)
        s2 = 1.0 / np.sqrt(D_HID)
        W1 = jax.random.uniform(k3, (D_IN, D_HID), dtype=jnp.float32, minval=-s1, maxval=s1)
        b1 = jax.random.uniform(k4, (D_HID,), dtype=jnp.float32, minval=-s1, maxval=s1)
        W2 = jax.random.uniform(k5, (D_HID, D_IN), dtype=jnp.float32, minval=-s2, maxval=s2)
        b2 = jax.random.uniform(k6, (D_IN,), dtype=jnp.float32, minval=-s2, maxval=s2)
        eps = jnp.zeros((1,), dtype=jnp.float32)
        return {'x': x, 'adj': adj, 'eps': eps, 'W1': W1, 'b1': b1, 'W2': W2, 'b2': b2}
    _L0_gnn_all = _L0_gnn_setup()
    _L0_gnn_in = {k: v for k, v in _L0_gnn_all.items() if k in ('eps', 'W1', 'b1', 'W2', 'b2')}
    del _L0_gnn_all

    def _L0_ffn_setup():
        import jax, jax.numpy as jnp
        import numpy as np
        B, S, D, E, H, K = (4, 2048, 128, 8, 256, 2)
        key = jax.random.key(seed)
        ks = jax.random.split(key, 6)
        x = jax.random.normal(ks[0], (B, S, D), jnp.float32)
        Wg = jax.random.normal(ks[1], (D, E), jnp.float32) * 0.02
        bg = jnp.zeros((E,), jnp.float32)
        W1 = jax.random.normal(ks[2], (E, D, H), jnp.float32) * 0.02
        b1 = jnp.zeros((E, H), jnp.float32)
        W2 = jax.random.normal(ks[3], (E, H, D), jnp.float32) * 0.02
        b2 = jnp.zeros((E, D), jnp.float32)
        return {'x': x, 'Wg': Wg, 'bg': bg, 'W1': W1, 'b1': b1, 'W2': W2, 'b2': b2}
    _L0_ffn_all = _L0_ffn_setup()
    _L0_ffn_in = {k: v for k, v in _L0_ffn_all.items() if k in ('Wg', 'bg', 'W1', 'b1', 'W2', 'b2')}
    del _L0_ffn_all

    def _L1_gnn_setup():
        import jax, jax.numpy as jnp
        import numpy as np
        GROUPS = [list(range(25)), [0, 1, 2, 3, 4, 5, 6, 7, 8], [0, 9, 10, 11, 12, 13, 14], [6, 7, 8, 12, 13, 14], [3, 4, 5, 9, 10, 11]]
        B, N, D_IN, D_HID = (4096, 25, 128, 256)

        def _graph_conv(x, adj, W, b):
            n = adj.shape[-1]
            A = adj + jnp.eye(n, dtype=adj.dtype)
            deg = jnp.sum(A, axis=-1)
            deg_safe = jnp.where(deg == 0, 1.0, deg)
            dinv = jnp.where(deg == 0, 0.0, deg_safe ** (-0.5))
            norm_adj = dinv[:, :, None] * A * dinv[:, None, :]
            support = jnp.einsum('bnd,de->bne', x, W)
            out = jnp.einsum('bnm,bme->bne', norm_adj, support) + b
            return jax.nn.relu(out)
        key = jax.random.key(seed)
        ks = jax.random.split(key, 7)
        s1 = float(np.sqrt(6.0 / (D_IN + D_HID)))
        s2 = float(np.sqrt(6.0 / (D_HID + D_IN)))
        return {'x': jax.random.normal(ks[0], (B, N, D_IN), dtype=jnp.float32), 'adj': jax.random.uniform(ks[1], (B, N, N), dtype=jnp.float32), 'W1': jax.random.uniform(ks[2], (5, D_IN, D_HID), jnp.float32, -s1, s1), 'b1': jnp.zeros((5, D_HID), dtype=jnp.float32), 'W2': jax.random.uniform(ks[3], (5, D_HID, D_IN), jnp.float32, -s2, s2), 'b2': jnp.zeros((5, D_IN), dtype=jnp.float32), 'fusion_w': jnp.ones((5,), dtype=jnp.float32)}
    _L1_gnn_all = _L1_gnn_setup()
    _L1_gnn_in = {k: v for k, v in _L1_gnn_all.items() if k in ('W1', 'b1', 'W2', 'b2', 'fusion_w')}
    del _L1_gnn_all

    def _L1_ffn_setup():
        import jax, jax.numpy as jnp
        import numpy as np
        NUM_EXPERTS = 8
        TOP_K = 2
        B, S, D = (8, 4096, 128)

        def _moe(tokens, router_w, w1, b1, w2, b2):
            N = tokens.shape[0]
            E = router_w.shape[0]
            logits = tokens.astype(jnp.float32) @ router_w.astype(jnp.float32).T
            probs = jax.nn.softmax(logits, axis=-1)
            rw, re = jax.lax.top_k(probs, TOP_K)
            if TOP_K > 1:
                rw = rw / jnp.maximum(rw.sum(-1, keepdims=True), 1e-12)
            rw = rw.astype(tokens.dtype)
            combine = jnp.zeros((N, E), tokens.dtype).at[jnp.arange(N)[:, None], re].set(rw)
            out = tokens
            for e in range(E):
                h = jax.nn.gelu(tokens @ w1[e] + b1[e], approximate=False)
                y = h @ w2[e] + b2[e]
                out = out + combine[:, e:e + 1] * y
            return out
        key = jax.random.key(seed)
        ks = jax.random.split(key, 4)
        scale = 1.0 / np.sqrt(D).astype(np.float32)
        return {'input_embeddings': jax.random.normal(ks[0], (B, S, D), jnp.float32), 'router_w': jax.random.normal(ks[1], (NUM_EXPERTS, D), jnp.float32) * scale, 'w1': jax.random.normal(ks[2], (NUM_EXPERTS, D, D), jnp.float32) * scale, 'b1': jnp.zeros((NUM_EXPERTS, D), jnp.float32), 'w2': jax.random.normal(ks[3], (NUM_EXPERTS, D, D), jnp.float32) * scale, 'b2': jnp.zeros((NUM_EXPERTS, D), jnp.float32)}
    _L1_ffn_all = _L1_ffn_setup()
    _L1_ffn_in = {k: v for k, v in _L1_ffn_all.items() if k in ('router_w', 'w1', 'b1', 'w2', 'b2')}
    del _L1_ffn_all
    return {'x': x, 'adj': adj, 'L0_gnn_eps': _L0_gnn_in['eps'], 'L0_gnn_W1': _L0_gnn_in['W1'], 'L0_gnn_b1': _L0_gnn_in['b1'], 'L0_gnn_W2': _L0_gnn_in['W2'], 'L0_gnn_b2': _L0_gnn_in['b2'], 'L0_ffn_Wg': _L0_ffn_in['Wg'], 'L0_ffn_bg': _L0_ffn_in['bg'], 'L0_ffn_W1': _L0_ffn_in['W1'], 'L0_ffn_b1': _L0_ffn_in['b1'], 'L0_ffn_W2': _L0_ffn_in['W2'], 'L0_ffn_b2': _L0_ffn_in['b2'], 'L1_gnn_W1': _L1_gnn_in['W1'], 'L1_gnn_b1': _L1_gnn_in['b1'], 'L1_gnn_W2': _L1_gnn_in['W2'], 'L1_gnn_b2': _L1_gnn_in['b2'], 'L1_gnn_fusion_w': _L1_gnn_in['fusion_w'], 'L1_ffn_router_w': _L1_ffn_in['router_w'], 'L1_ffn_w1': _L1_ffn_in['w1'], 'L1_ffn_b1': _L1_ffn_in['b1'], 'L1_ffn_w2': _L1_ffn_in['w2'], 'L1_ffn_b2': _L1_ffn_in['b2']}

def reference(x, adj, L0_gnn_eps, L0_gnn_W1, L0_gnn_b1, L0_gnn_W2, L0_gnn_b2, L0_ffn_Wg, L0_ffn_bg, L0_ffn_W1, L0_ffn_b1, L0_ffn_W2, L0_ffn_b2, L1_gnn_W1, L1_gnn_b1, L1_gnn_W2, L1_gnn_b2, L1_gnn_fusion_w, L1_ffn_router_w, L1_ffn_w1, L1_ffn_b1, L1_ffn_w2, L1_ffn_b2):
    import jax
    import jax.numpy as jnp

    def _L0_gnn_ref(x, adj, eps, W1, b1, W2, b2):
        import jax, jax.numpy as jnp
        import numpy as np
        D_IN = 128
        D_HID = 256
        aggregated = jnp.einsum('bnm,bmd->bnd', adj, x)
        h = (1.0 + eps) * x + aggregated
        h = jax.nn.relu(h @ W1 + b1)
        return h @ W2 + b2

    def _L0_ffn_ref(x, Wg, bg, W1, b1, W2, b2):
        import jax, jax.numpy as jnp
        import numpy as np
        B, S, D, E, H, K = (4, 2048, 128, 8, 256, 2)
        Bv, Sv, Dv = x.shape
        gate_scores = x @ Wg + bg
        _, idx = jax.lax.top_k(gate_scores, K)
        mask = jax.nn.one_hot(idx, E, dtype=x.dtype).sum(axis=-2)
        xf = x.reshape(-1, Dv)
        mf = mask.reshape(-1, E)
        h = jax.nn.gelu(jnp.einsum('td,edh->teh', xf, W1) + b1[None], approximate=False)
        y = jnp.einsum('teh,ehd->ted', h, W2) + b2[None]
        out = jnp.einsum('ted,te->td', y, mf)
        return out.reshape(Bv, Sv, Dv)

    def _L1_gnn_ref(x, adj, W1, b1, W2, b2, fusion_w):
        import jax, jax.numpy as jnp
        import numpy as np
        GROUPS = [list(range(25)), [0, 1, 2, 3, 4, 5, 6, 7, 8], [0, 9, 10, 11, 12, 13, 14], [6, 7, 8, 12, 13, 14], [3, 4, 5, 9, 10, 11]]
        B, N, D_IN, D_HID = (4096, 25, 128, 256)

        def _graph_conv(x, adj, W, b):
            n = adj.shape[-1]
            A = adj + jnp.eye(n, dtype=adj.dtype)
            deg = jnp.sum(A, axis=-1)
            deg_safe = jnp.where(deg == 0, 1.0, deg)
            dinv = jnp.where(deg == 0, 0.0, deg_safe ** (-0.5))
            norm_adj = dinv[:, :, None] * A * dinv[:, None, :]
            support = jnp.einsum('bnd,de->bne', x, W)
            out = jnp.einsum('bnm,bme->bne', norm_adj, support) + b
            return jax.nn.relu(out)
        norm_w = jax.nn.softmax(fusion_w)
        fused = jnp.zeros_like(x)
        for g, idx_list in enumerate(GROUPS):
            idx = jnp.asarray(idx_list)
            x_g = x[:, idx, :]
            adj_g = adj[:, idx][:, :, idx]
            h = _graph_conv(x_g, adj_g, W1[g], b1[g])
            out_g = _graph_conv(h, adj_g, W2[g], b2[g])
            fused = fused.at[:, idx, :].add(norm_w[g] * out_g)
        return fused

    def _L1_ffn_ref(input_embeddings, router_w, w1, b1, w2, b2):
        import jax, jax.numpy as jnp
        import numpy as np
        NUM_EXPERTS = 8
        TOP_K = 2
        B, S, D = (8, 4096, 128)

        def _moe(tokens, router_w, w1, b1, w2, b2):
            N = tokens.shape[0]
            E = router_w.shape[0]
            logits = tokens.astype(jnp.float32) @ router_w.astype(jnp.float32).T
            probs = jax.nn.softmax(logits, axis=-1)
            rw, re = jax.lax.top_k(probs, TOP_K)
            if TOP_K > 1:
                rw = rw / jnp.maximum(rw.sum(-1, keepdims=True), 1e-12)
            rw = rw.astype(tokens.dtype)
            combine = jnp.zeros((N, E), tokens.dtype).at[jnp.arange(N)[:, None], re].set(rw)
            out = tokens
            for e in range(E):
                h = jax.nn.gelu(tokens @ w1[e] + b1[e], approximate=False)
                y = h @ w2[e] + b2[e]
                out = out + combine[:, e:e + 1] * y
            return out
        b, s, d = input_embeddings.shape
        tokens = input_embeddings.reshape(b * s, d)
        return _moe(tokens, router_w, w1, b1, w2, b2).reshape(b, s, d)
    x = x + _L0_gnn_ref(_layernorm(x, axis=-1), adj, L0_gnn_eps, L0_gnn_W1, L0_gnn_b1, L0_gnn_W2, L0_gnn_b2)
    x = x + _L0_ffn_ref(_layernorm(x, axis=-1), L0_ffn_Wg, L0_ffn_bg, L0_ffn_W1, L0_ffn_b1, L0_ffn_W2, L0_ffn_b2)
    x = x + _L1_gnn_ref(_layernorm(x, axis=-1), adj, L1_gnn_W1, L1_gnn_b1, L1_gnn_W2, L1_gnn_b2, L1_gnn_fusion_w)
    x = x + _L1_ffn_ref(_layernorm(x, axis=-1), L1_ffn_router_w, L1_ffn_w1, L1_ffn_b1, L1_ffn_w2, L1_ffn_b2)
    return x

_drawn_inputs = setup_inputs


def setup_inputs(seed=0):
    import zlib

    import numpy as np

    out = dict(_drawn_inputs(seed))
    spreads = {'L0_ffn_bg': (0.0, 0.1),
     'L0_ffn_b1': (0.0, 0.1),
     'L0_ffn_b2': (0.0, 0.1),
     'L1_gnn_b1': (0.0, 0.682),
     'L1_gnn_b2': (0.0, 0.562),
     'L1_gnn_fusion_w': (1.0, 0.6),
     'L1_ffn_b1': (0.0, 0.333),
     'L1_ffn_b2': (0.0, 0.1)}
    factors = {}
    for name, (base, spread) in spreads.items():
        noise = np.random.default_rng([zlib.crc32(name.encode()), seed]).standard_normal(out[name].shape)
        drawn = base * np.exp(spread * noise) if base else spread * noise
        out[name] = jnp.asarray(drawn.astype(out[name].dtype))
    for name, factor in factors.items():
        out[name] = (out[name] * factor).astype(out[name].dtype)
    return out
```

```python
from contextlib import ExitStack

import concourse.bass as bass
from concourse import mybir

F32 = mybir.dt.float32
F32R = mybir.dt.float32r
BF16 = mybir.dt.bfloat16
ALU = mybir.AluOpType
ACT = mybir.ActivationFunctionType
AX = mybir.AxisListType.X

P = 128
B = 64
G = 4
T = G * P
GROUPS = B // G
E = 8
C0 = 16
C1 = 8
Z_RING = 3
RING = 6
LAG = 4
PARTS = 3
ONES = PARTS * E
NODES = [list(range(25)), [0, 1, 2, 3, 4, 5, 6, 7, 8], [0, 9, 10, 11, 12, 13, 14], [6, 7, 8, 12, 13, 14],
         [3, 4, 5, 9, 10, 11]]
FIRST = [sum(len(n) for n in NODES[:k]) for k in range(len(NODES))]
USED = sum(len(n) for n in NODES)
S = 64
PAIRS = B // 2
EPS = 1e-5
FAR = 3e38


def program(nc, a, out):
    ctx = ExitStack()
    with ctx:
        def sb(name, shape, dt=F32):
            return ctx.enter_context(nc.sbuf_tensor(name, shape, dt))

        def psum(name):
            return ctx.enter_context(nc.psum_tensor(name, [P, T], F32))

        def sem(name):
            return ctx.enter_context(nc.semaphore(name))

        ident = sb("ident", [P, P])
        identb = sb("identb", [P, P], BF16)
        rank = sb("rank", [P, E])
        eye_eps = sb("eye_eps", [P, G, P])
        eps_col = sb("eps_col", [P, 1])
        pow_half = sb("pow_half", [P, G])
        pow_base = sb("pow_base", [P, G * E])
        g0_w1 = sb("g0_w1", [P, 2 * P])
        g0_w2 = sb("g0_w2", [P, 2, P])
        g0_b1 = sb("g0_b1", [P, 2])
        g0_b2 = sb("g0_b2", [P, P])
        gate_w = sb("gate_w", [P, 2, E])
        gate_hi = sb("gate_hi", [P, 2, E], F32R)
        gate_lo = sb("gate_lo", [P, 2, E], F32R)
        gate_b = sb("gate_b", [P, E])
        stage = sb("stage", [P, 2, 2048])
        w_hi = sb("w_hi", [P, 3, 2048], F32R)
        w_lo = sb("w_lo", [P, 3, 2048], F32R)
        e0_b1 = sb("e0_b1", [P, C0])
        e1_b1 = sb("e1_b1", [P, C1])
        e_b2 = sb("e_b2", [P, 2, P])
        b2_rest = sb("b2_rest", [P, 2, P])
        b2_rest2 = sb("b2_rest2", [P, 2, P])
        b2_part = sb("b2_part", [P, PARTS, 2, P], BF16)
        part_rows = sb("part_rows", [P, PARTS])
        b2_mix = sb("b2_mix", [P, PARTS, P])
        e0_b2 = sb("e0_b2", [P, P], BF16)
        shut_rows = sb("shut_rows", [P, E])
        pick_rows = sb("pick_rows", [P, E])
        shut = sb("shut", [P, E, P], BF16)
        pick = sb("pick", [P, E, P], BF16)
        g1_w1 = sb("g1_w1", [P, 5, 2, P])
        g1_w2 = sb("g1_w2", [P, 5, 2, P])
        g1_b1 = sb("g1_b1", [P, 2, S])
        g1_b2 = sb("g1_b2", [P, P])
        slot_token = sb("slot_token", [P, 2, P])
        slot_group = sb("slot_group", [P, 5])
        fuse_w = sb("fuse_w", [P, 5])
        fuse = sb("fuse", [P, 2, P])
        fw = [sb(f"fw{n}", [P, 5]) for n in range(4)]
        fw_col = [sb(f"fw_col{n}", [P, 1]) for n in range(4)]

        x_in = sb("x_in", [P, G, P])
        adj_in = sb("adj_in", [P, G, P])
        adj_eye = sb("adj_eye", [P, G, P])
        x_b2 = sb("x_b2", [P, G, P])
        agg0 = sb("agg0", [P, T])
        hid0 = sb("hid0", [P, 2, T])
        x1_new = sb("x1_new", [P, G, P])
        x1 = sb("x1", [P, G, P])
        stats = [sb(f"stats{n}", [P, G, 6]) for n in range(4)]
        mean_var = [sb(f"mean_var{n}", [P, G, 2]) for n in range(4)]
        var_eps = [sb(f"var_eps{n}", [P, G]) for n in range(4)]
        minus_mean = [sb(f"minus_mean{n}", [P, G]) for n in range(4)]
        shift = [sb(f"shift{n}", [P, G]) for n in range(4)]
        rstd = [sb(f"rstd{n}", [P, G]) for n in range(4)]
        normed = [sb(f"normed{n}", [P, G, P]) for n in range(4)]
        xt_hi = [sb(f"xt_hi{n}", [P, T], F32R) for n in range(2)]
        xt_lo = [sb(f"xt_lo{n}", [P, T], F32R) for n in range(2)]
        score = [sb(f"score{n}", [P, G, E]) for n in range(2)]
        best = [sb(f"best{n}", [P, G]) for n in range(2)]
        equal = [sb(f"equal{n}", [P, G, E]) for n in range(2)]
        ranked = [sb(f"ranked{n}", [P, G, E]) for n in range(2)]
        top = [sb(f"top{n}", [P, G]) for n in range(2)]
        first = [sb(f"first{n}", [P, G, E]) for n in range(2)]
        second = [sb(f"second{n}", [P, G, E]) for n in range(2)]
        left = [sb(f"left{n}", [P, G, E]) for n in range(2)]
        soft = [sb(f"soft{n}", [P, G, E]) for n in range(7)]
        soft_col = [sb(f"soft_col{n}", [P, G]) for n in range(6)]
        rows = [sb(f"rows{n}", [P, G, P], BF16) for n in range(2)]
        rows_t = [sb(f"rows_t{n}", [P, T], BF16) for n in range(2)]
        hid = sb("hid", [P, RING, T])
        h_hi = sb("h_hi", [P, RING, T], F32R)
        h_lo = sb("h_lo", [P, RING, T], F32R)
        y0_t = sb("y0_t", [P, T])
        y1_t = sb("y1_t", [P, T])
        x2 = sb("x2", [P, G, P])
        x3 = sb("x3", [P, G, P])
        x3_tokens = sb("x3_tokens", [P, G, P])
        x_out = sb("x_out", [P, G, P])
        block_in = sb("block_in", [P, 2, P])
        block = sb("block", [P, 2, P])
        degree = sb("degree", [P, 2])
        no_degree = sb("no_degree", [P, 2])
        safe_degree = sb("safe_degree", [P, 2])
        raised = sb("raised", [P, 2])
        has_degree = sb("has_degree", [P, 2])
        dinv = sb("dinv", [P, 2])
        block_row = sb("block_row", [P, 2, P])
        norm_t = sb("norm_t", [P, 2, P])
        norm_tok = sb("norm_tok", [P, 2, 2, S])
        agg1 = sb("agg1", [P, G, S])
        hid1_b = sb("hid1_b", [P, 2, G, S])
        hid1 = sb("hid1", [P, 2, G, S])
        supp_t = sb("supp_t", [P, G, S])
        supp = sb("supp", [P, 2, P])
        conv_b = sb("conv_b", [P, 2, P])
        conv = sb("conv", [P, 2, P])

        z = [psum(f"z{n}") for n in range(Z_RING)]
        y0 = psum("y0")
        y1 = psum("y1")
        spread = psum("spread")
        pa = psum("pa")
        pb = psum("pb")

        names = """x_loaded adj_loaded block_loaded small_loaded late_loaded bf16_consts w_loaded0 w_loaded1 w_loaded2 w_hi_done w_lo_done
            consts_set pool_consts gate_w_hi gate_w_lo eye_eps_done eps_done b2_step e0_b2_done w_split
            fuse_step fuse_d fuse_pow fuse_done
            adj_done x_b2_done agg0_ps agg0_done hid0_ps hid0_done x1_ps x1_new_done x1_done
            xt_ps0 xt_ps1 xt_hi0 xt_hi1 xt_lo0 xt_lo1 score_ps0 score_ps1 score_done0 score_done1
            pick_step0 pick_step1 soft_d soft_e soft_step
            rows_done0 rows_done1 rows_ps0 rows_ps1 rows_t0 rows_t1
            z_ready gelu_done hi_done lo_done y_done spread_ready weighted_done
            y0_t y0_back x2_done y1_t y1_back out_done out_stored
            block_eye deg_step deg_pow dinv_done block_row_done norm_ps norm_t_done tok_ps norm_tok_done
            agg1_ps agg1_done hid1_ps hid1_b_done hid1_done supp_t_ps supp_t_done supp_ps supp_done
            conv_ps conv_b_done conv_done fuse_ps x3_done x3_tokens_done dve_held pool_held sp_held""".split()
        s = {n: sem(n) for n in names}
        ln = [{k: sem(f"ln{n}_{k}") for k in ("stats", "moments", "var", "minus", "rstd", "shift", "normed")} for n in range(4)]

        def after(eng, name, value):
            if not (isinstance(value, int) and value <= 0):
                eng.wait_ge(s[name], value)

        def wide(ap, dim, n):
            return ap.unsqueeze(dim).to_broadcast([*ap.shape[:dim], n, *ap.shape[dim:]])

        def chain(eng, name, base):
            done = [base]

            def link(ins):
                done[0] = done[0] + 1
                ins.then_inc(s[name], 1)
                eng.wait_ge(s[name], done[0])
            return link

        block_ctx = ctx.enter_context(nc.Block())

        def schedule(eng, late, early, start, end):
            turn = C0 + C1
            start()
            early(-2, 0, q=False, fin=False)
            late(-1, C0, f1=False)
            early(-1, C0, fin=False)
            late(0, 2 * C0)
            early(0, 2 * C0 + C1)
            with eng.Fori(1, GROUPS - 3) as i:
                late(i, i * turn + 2 * C0)
                early(i, i * turn + 2 * C0 + C1)
            i = GROUPS - 3
            late(i, i * turn + 2 * C0)
            early(i, i * turn + 2 * C0 + C1, pre=False)
            i = GROUPS - 2
            late(i, i * turn + 2 * C0, pre=False)
            early(i, i * turn + 2 * C0 + C1, f0=False, pre=False)
            late(i + 1, i * turn + 2 * C0 + C1, pre=False, back=False)
            end(i + 1, i * turn + 2 * C0 + 2 * C1)

        assert (C0 + C1) % RING == 0 and RING % Z_RING == 0 and LAG + 2 <= RING

        def late_ring(i):
            return {-1: C0, GROUPS - 1: 2 * C0 + C1}.get(i if isinstance(i, int) else 0, 2 * C0) % RING

        def early_ring(i):
            return {-2: 0, -1: C0}.get(i if isinstance(i, int) else 0, 2 * C0 + C1) % RING

        SMALL = [(ident[:, :], "ident"), (eps_col[:, :], "eps"), (g0_w1[:, :], "g0_w1"),
                 (g0_w2[:, :, :], "g0_w2"), (g0_b1[:, :], "g0_b1"), (g0_b2[:, :], "g0_b2"),
                 (gate_w[:, :, :], "gate_w"), (gate_b[:, :], "gate_b"), (rank[:, :], "rank"),
                 (shut_rows[:, :], "shut_rows"), (pick_rows[:, :], "pick_rows"), (e0_b1[:, :], "e0_b1"), (e_b2[:, :, :], "e_b2"),
                 (part_rows[:, :], "part_rows")]
        LATE = [(fuse_w[:, :], "fuse_w"), (slot_group[:, :], "slot_group"), (slot_token[:, :, :], "slot_token"),
                (g1_w1[:, :, :, :], "g1_w1"), (g1_w2[:, :, :, :], "g1_w2"), (g1_b1[:, :, :], "g1_b1"),
                (g1_b2[:, :], "g1_b2"), (e1_b1[:, :], "e1_b1")]

        @block_ctx.sync
        def _(sp):
            def held():
                sp.sem_inc(s["sp_held"], 1)

            def load_x(n):
                after(sp, "x_b2_done", n)
                held()
                if not (isinstance(n, int) and n == 0):
                    sp.wait_ge(ln[0]["normed"], n * G)
                held()
                sp.dma_start(x_in[:, :, :], a["x"][:, bass.ds(n * G, G), :]).then_inc(s["x_loaded"], 16)
                after(sp, "adj_done", n)
                held()
                sp.dma_start(adj_in[:, :, :], a["adj"][:, bass.ds(n * G, G), :]).then_inc(s["adj_loaded"], 16)

            def load_block(n):
                after(sp, "block_eye", n)
                held()
                sp.dma_start(block_in[:, :, :], a["block"][:, bass.ds(n * 2, 2), :]).then_inc(s["block_loaded"], 16)

            load_x(0)
            sp.dma_start(stage[:, 0, :], a["e0_w1"]).then_inc(s["w_loaded0"], 16)
            sp.dma_start(stage[:, 1, :], a["e0_w2"]).then_inc(s["w_loaded1"], 16)
            load_block(0)
            load_x(1)
            sp.wait_ge(s["w_lo_done"], 1)
            sp.dma_start(stage[:, 0, :], a["e1_w"]).then_inc(s["w_loaded2"], 16)
            load_x(2)
            with sp.Fori(3, GROUPS) as n:
                load_x(n)
                load_block(n - 2)
            load_block(GROUPS - 2)
            load_block(GROUPS - 1)

        @block_ctx.scalar
        def _(act):
            def copy(dst, src):
                return nc.scalar.activation(dst, src, ACT.Copy)

            def gelu(c, ring, bias):
                act.wait_ge(s["z_ready"], c + 1)
                after(act, "lo_done", c - RING + 1)
                nc.scalar.activation(hid[:, ring, :], z[ring % Z_RING][:, :], ACT.Gelu, bias=bias).then_inc(s["gelu_done"], 1)

            def agg0_copy(n):
                act.wait_ge(s["agg0_ps"], n + 1)
                after(act, "hid0_ps", n * 2)
                copy(agg0[:, :], pa[:, :]).then_inc(s["agg0_done"], 1)

            def relu0(n, c):
                act.wait_ge(s["hid0_ps"], n * 2 + c + 1)
                after(act, "x1_ps", n)
                nc.scalar.activation(hid0[:, c, :], pa[:, :], ACT.Relu, bias=g0_b1[:, c:c + 1])\
                    .then_inc(s["hid0_done"], 1)

            def keep_x1(n):
                act.wait_ge(s["x1_new_done"], n + 1)
                after(act, "x2_done", n)
                copy(x1[:, :, :], x1_new[:, :, :]).then_inc(s["x1_done"], 1)

            def xt_copy(k, n, ps):
                act.wait_ge(s[f"xt_ps{k}"], n + 1)
                after(act, f"score_ps{k}", n)
                copy(xt_hi[k][:, :], ps[:, :]).then_inc(s[f"xt_hi{k}"], 1)

            def rows_copy(k, n):
                act.wait_ge(s[f"rows_ps{k}"], n + 1)
                copy(rows_t[k][:, :], pb[:, :].bitcast(BF16)[:, 0:T]).then_inc(s[f"rows_t{k}"], 1)

            def y_copy(k, n, c):
                act.wait_ge(s["y_done"], c)
                after(act, f"y{k}_back", n)
                copy((y1_t if k else y0_t)[:, :], (y1 if k else y0)[:, :]).then_inc(s[f"y{k}_t"], 1)

            def norm_tok_copy(n):
                act.wait_ge(s["tok_ps"], n + 1)
                after(act, "agg1_ps", n)
                copy(norm_tok[:, :, :, :].rearrange("p a b c -> p (a b c)"), pb[:, 0:G * S])\
                    .then_inc(s["norm_tok_done"], 1)

            def agg1_copy(n):
                act.wait_ge(s["agg1_ps"], n + 1)
                after(act, "hid1_ps", n)
                copy(agg1[:, :, 0:USED], pa[:, 0:G * S].rearrange("p (b n) -> p b n", b=G)[:, :, 0:USED])\
                    .then_inc(s["agg1_done"], 1)

            def relu1(n):
                act.wait_ge(s["hid1_b_done"], n * 2 + 2)
                after(act, "supp_t_ps", n)
                nc.scalar.activation(hid1[:, :, :, 0:USED].rearrange("p c b n -> p (c b) n"),
                                     hid1_b[:, :, :, 0:USED].rearrange("p c b n -> p (c b) n"),
                                     ACT.Relu).then_inc(s["hid1_done"], 1)

            def supp_t_copy(n):
                act.wait_ge(s["supp_t_ps"], n + 1)
                after(act, "supp_ps", n)
                copy(supp_t[:, :, 0:USED], pb[:, 0:G * S].rearrange("p (b n) -> p b n", b=G)[:, :, 0:USED])\
                    .then_inc(s["supp_t_done"], 1)

            def supp_copy(n):
                act.wait_ge(s["supp_ps"], n + 1)
                after(act, "conv_ps", n)
                copy(supp[:, :, :].rearrange("p a d -> p (a d)"), pb[:, 0:2 * P]).then_inc(s["supp_done"], 1)

            def relu2(n):
                act.wait_ge(s["conv_b_done"], n + 1)
                after(act, "fuse_ps", n)
                nc.scalar.activation(conv[:, :, :], conv_b[:, :, :], ACT.Relu).then_inc(s["conv_done"], 1)

            def store(n):
                act.wait_ge(s["out_done"], n + 1)
                act.dma_start(out[:, bass.ds(n * G, G), :], x_out[:, :, :]).then_inc(s["out_stored"], 16)

            def split_hi(k):
                act.wait_ge(s[f"w_loaded{k}"], 16)
                copy(w_hi[:, k, :], stage[:, k % 2, :]).then_inc(s["w_hi_done"], 1)

            def norm_apply(k, n, src, used):
                act.wait_ge(ln[k]["shift"], n + 1)
                after(act, used, n)
                for b in range(G):
                    nc.scalar.activation(normed[k][:, b, :], src[:, b, :], ACT.Identity, bias=shift[k][:, b:b + 1],
                                         scale=rstd[k][:, b:b + 1]).then_inc(ln[k]["normed"], 1)

            def start():
                for dst, name in SMALL:
                    act.dma_start(dst, a[name]).then_inc(s["small_loaded"], 16)
                for dst, name in LATE:
                    act.dma_start(dst, a[name]).then_inc(s["late_loaded"], 16)
                norm_apply(0, 0, x_in, "agg0_ps")
                act.wait_ge(s["small_loaded"], 16 * len(SMALL))
                copy(gate_hi[:, :, :], gate_w[:, :, :]).then_inc(s["gate_w_hi"], 1)
                copy(identb[:, :], ident[:, :]).then_inc(s["bf16_consts"], 1)
                copy(shut[:, :, :], wide(shut_rows[:, :], 2, P)).then_inc(s["bf16_consts"], 1)
                copy(pick[:, :, :], wide(pick_rows[:, :], 2, P)).then_inc(s["bf16_consts"], 1)
                agg0_copy(0)
                split_hi(0)
                relu0(0, 0)
                relu0(0, 1)
                split_hi(1)
                keep_x1(0)
                norm_apply(1, 0, x1_new, "xt_ps0")
                xt_copy(0, 0, pa)
                rows_copy(0, 0)

            def early(i, c0, f0=True, q=True, pre=True, fin=True):
                n, m, r = i + 1, i + 3, early_ring(i)
                for t in range(C0):
                    if f0:
                        gelu(c0 + t, (r + t) % RING, e0_b1[:, t:t + 1])
                    if t == 0 and not q:
                        act.wait_ge(s["late_loaded"], 16 * len(LATE))
                        split_hi(2)
                    if t == 1 and q:
                        agg1_copy(n)
                    if t == 3 and q:
                        relu1(n)
                    if t == 4 and fin:
                        y_copy(1, i, c0)
                    if t == 4 and q:
                        supp_t_copy(n)
                    if t == 5 and pre:
                        norm_apply(0, m, x_in, "agg0_ps")
                    if t == 5 and q:
                        supp_copy(n)
                    if t == 6 and pre:
                        agg0_copy(m)
                    if t == 8 and q:
                        relu2(n)
                    if t == 8 and pre:
                        relu0(m, 0)
                    if t == 8 and fin:
                        store(i)
                    if t == 10 and pre:
                        relu0(m, 1)
                    if t == 11 and q:
                        norm_apply(3, n, x3, "xt_ps1")
                    if t == 12 and q:
                        xt_copy(1, n, pb)
                    if t == 14 and pre:
                        norm_apply(1, m, x1_new, "xt_ps0")

            def late(i, c0, f1=True, pre=True, back=True):
                r = late_ring(i)
                for t in range(C1):
                    if f1:
                        gelu(c0 + t, (r + t) % RING, e1_b1[:, t:t + 1])
                    if t == 0 and f1:
                        rows_copy(1, i)
                    if t == 1 and pre:
                        xt_copy(0, i + 2, pa)
                    if t == 4 and back:
                        y_copy(0, i + 1, c0)
                    if t == 6 and pre:
                        rows_copy(0, i + 2)
                    if t == 6 and back:
                        norm_apply(2, i + 1, x2, "agg1_ps")
                    if t == 7 and pre:
                        keep_x1(i + 2)
                    if t == 7 and back:
                        norm_tok_copy(i + 1)

            def end(i, c):
                y_copy(1, i, c)
                store(i)
                act.wait_ge(s["out_stored"], 16 * GROUPS)

            schedule(act, late, early, start, end)

        @block_ctx.gpsimd
        def _(pool):
            def held():
                pool.sem_inc(s["pool_held"], 1)

            def hi0(c, ring):
                pool.wait_ge(s["gelu_done"], c + 1)
                after(pool, "y_done", c - RING + 1)
                held()
                nc.gpsimd.tensor_scalar(h_hi[:, ring, :], hid[:, ring, :], 1.0, 0.0, ALU.mult, ALU.add)\
                    .then_inc(s["hi_done"], 1)

            def hi1(c, ring, done):
                pool.wait_ge(s["weighted_done"], done)
                after(pool, "y_done", c - RING + 1)
                held()
                nc.gpsimd.tensor_scalar(h_hi[:, ring, :], hid[:, ring, :], 1.0, 0.0, ALU.mult, ALU.add)\
                    .then_inc(s["hi_done"], 1)

            def rstd_pow(k, n):
                pool.wait_ge(ln[k]["var"], n + 1)
                if not (isinstance(n, int) and n == 0):
                    pool.wait_ge(ln[k]["normed"], n * G)
                nc.gpsimd.tensor_tensor(rstd[k][:, :], var_eps[k][:, :], pow_half[:, :], ALU.pow)\
                    .then_inc(ln[k]["rstd"], 1)
                pool.wait_ge(ln[k]["rstd"], n + 1)
                nc.gpsimd.tensor_tensor(shift[k][:, :], minus_mean[k][:, :], rstd[k][:, :], ALU.mult)\
                    .then_inc(ln[k]["shift"], 1)

            def adj_add(n):
                pool.wait_ge(s["adj_loaded"], n * 16 + 16)
                after(pool, "agg0_ps", n)
                nc.gpsimd.tensor_tensor(adj_eye[:, :, :], adj_in[:, :, :], eye_eps[:, :, :], ALU.add)\
                    .then_inc(s["adj_done"], 1)

            def x_b2_add(n):
                pool.wait_ge(s["x_loaded"], n * 16 + 16)
                after(pool, "x1_new_done", n)
                nc.gpsimd.tensor_tensor(x_b2[:, :, :], x_in[:, :, :], wide(g0_b2[:, :], 1, G), ALU.add)\
                    .then_inc(s["x_b2_done"], 1)

            def x3_tokens_add(n):
                pool.wait_ge(ln[3]["normed"], n * G + G)
                after(pool, "out_done", n)
                nc.gpsimd.tensor_tensor(x3_tokens[:, :, :], x3[:, :, :], normed[3][:, :, :], ALU.add)\
                    .then_inc(s["x3_tokens_done"], 1)

            def start():
                nc.gpsimd.memset(pow_half[:, :], -0.5).then_inc(s["pool_consts"], 1)
                nc.gpsimd.memset(pow_base[:, :], 2.718281828459045).then_inc(s["pool_consts"], 1)
                nc.gpsimd.memset(supp_t[:, :, :], 0.0).then_inc(s["consts_set"], 1)
                for k in range(2):
                    nc.gpsimd.memset(rows[k][:, :, :], 0.0).then_inc(s["consts_set"], 1)
                pool.wait_ge(s["consts_set"], 3)
                nc.gpsimd.memset(rows[0][:, :, ONES:ONES + E], 1.0).then_inc(s["consts_set"], 1)
                pool.wait_ge(s["pool_consts"], 2)
                pool.wait_ge(s["small_loaded"], 16 * len(SMALL))
                rstd_pow(0, 0)
                pool.wait_ge(s["eye_eps_done"], 1)
                adj_add(0)
                x_b2_add(0)
                rstd_pow(1, 0)

            def early(i, c0, f0=True, q=True, pre=True, fin=True):
                n, m, r = i + 1, i + 3, early_ring(i)
                if fin:
                    hi1(c0 - 1, (r - 1) % RING, i * C1 + C1)
                for t in range(C0):
                    if f0:
                        hi0(c0 + t, (r + t) % RING)
                    if t == 1 and not q:
                        pool.wait_ge(s["fuse_d"], 1)
                        nc.gpsimd.tensor_tensor(fw[2][:, :], pow_base[:, 0:5], fw[1][:, :], ALU.pow)\
                            .then_inc(s["fuse_pow"], 1)
                    if t == 2 and pre:
                        adj_add(m)
                    if t == 4 and pre:
                        rstd_pow(0, m)
                    if t == 6 and pre:
                        x_b2_add(m)
                    if t == 10 and q:
                        rstd_pow(3, n)
                    if t == 12 and pre:
                        rstd_pow(1, m)
                    if t == 13 and q:
                        x3_tokens_add(n)
                    if t == 14 and q:
                        pool.wait_ge(s["soft_d"], n + 1)
                        nc.gpsimd.tensor_tensor(soft_col[1][:, :], pow_base[:, 0:G], soft_col[0][:, :], ALU.pow)\
                            .then_inc(s["soft_e"], 1)

            def late(i, c0, f1=True, pre=True, back=True):
                r = late_ring(i)
                for t in range(C1):
                    if f1 and t > 0:
                        hi1(c0 + t - 1, (r + t - 1) % RING, i * C1 + t)
                    if t == 3 and back:
                        pool.wait_ge(s["deg_step"], (i + 1) * 3 + 3)
                        nc.gpsimd.tensor_tensor(raised[:, :], safe_degree[:, :], pow_half[:, 0:2], ALU.pow)\
                            .then_inc(s["deg_pow"], 1)
                    if t == 5 and back:
                        rstd_pow(2, i + 1)

            def end(i, c):
                hi1(c - 1, (late_ring(i) + C1 - 1) % RING, i * C1 + C1)

            schedule(pool, late, early, start, end)

        @block_ctx.vector
        def _(dve):
            V = nc.vector

            def held():
                dve.sem_inc(s["dve_held"], 1)

            def lo(c, ring):
                dve.wait_ge(s["hi_done"], c + 1)
                V.tensor_tensor(h_lo[:, ring, :], hid[:, ring, :], h_hi[:, ring, :].bitcast(F32), ALU.subtract)\
                    .then_inc(s["lo_done"], 1)

            def weigh(c, ring, done):
                dve.wait_ge(s["gelu_done"], c + 1)
                dve.wait_ge(s["spread_ready"], done)
                V.tensor_tensor(hid[:, ring, :], hid[:, ring, :], spread[:, :], ALU.mult)\
                    .then_inc(s["weighted_done"], 1)

            def norm_stats(k, n, src):
                for b in range(G):
                    V.bn_stats(stats[k][:, b, :], src[:, b, :]).then_inc(ln[k]["stats"], 1)
                dve.wait_ge(ln[k]["stats"], n * G + G)
                held()
                for b in range(G):
                    V.bn_aggr(mean_var[k][:, b, :], stats[k][:, b, :]).then_inc(ln[k]["moments"], 1)
                dve.wait_ge(ln[k]["moments"], n * G + G)
                V.tensor_scalar(minus_mean[k][:, :], mean_var[k][:, :, 0], -1.0, None, ALU.mult)\
                    .then_inc(ln[k]["minus"], 1)
                V.tensor_scalar(var_eps[k][:, :], mean_var[k][:, :, 1], EPS, None, ALU.add).then_inc(ln[k]["var"], 1)

            def xt_rest(k, n, ps):
                dve.wait_ge(s[f"xt_hi{k}"], n + 1)
                V.tensor_tensor(xt_lo[k][:, :], ps[:, :], xt_hi[k][:, :].bitcast(F32), ALU.subtract)\
                    .then_inc(s[f"xt_lo{k}"], 1)

            def choose(k, n):
                link = chain(dve, f"pick_step{k}", n * 11)
                dve.wait_ge(s[f"score_done{k}"], n + 1)
                for step, (src, hot) in enumerate(((score[k], first[k]), (left[k], second[k]))):
                    high = best[k] if step == 0 else soft_col[4 + k]
                    link(V.tensor_reduce(high[:, :], src[:, :, :], AX, ALU.max))
                    link(V.tensor_tensor(equal[k][:, :, :], src[:, :, :], wide(high[:, :], 2, E), ALU.is_equal))
                    link(V.tensor_tensor(ranked[k][:, :, :], equal[k][:, :, :], wide(rank[:, :], 1, G), ALU.mult))
                    link(V.tensor_reduce(top[k][:, :], ranked[k][:, :, :], AX, ALU.max))
                    link(V.tensor_tensor(hot[:, :, :], ranked[k][:, :, :], wide(top[k][:, :], 2, E), ALU.is_equal))
                    if step == 0:
                        link(V.scalar_tensor_tensor(out=left[k][:, :, :], in0=hot[:, :, :], scalar=-FAR,
                                                    in1=src[:, :, :], op0=ALU.mult, op1=ALU.add))

            def gate_rows(n):
                dve.wait_ge(s["score_ps0"], n + 1)
                V.tensor_tensor(score[0][:, :, :], pb[:, 0:G * E].rearrange("p (b e) -> p b e", b=G),
                                wide(gate_b[:, :], 1, G), ALU.add).then_inc(s["score_done0"], 1)
                choose(0, n)
                after(dve, "rows_ps0", n)
                V.tensor_tensor(rows[0][:, :, 0:ONES].rearrange("p b (k e) -> p b k e", k=PARTS),
                                wide(first[0][:, :, :], 2, PARTS), wide(second[0][:, :, :], 2, PARTS), ALU.add)\
                    .then_inc(s["rows_done0"], 1)

            def router_choose(n):
                dve.wait_ge(s["score_ps1"], n + 1)
                V.tensor_copy(score[1][:, :, :], pa[:, 0:G * E].rearrange("p (b e) -> p b e", b=G))\
                    .then_inc(s["score_done1"], 1)
                choose(1, n)
                V.tensor_tensor(soft_col[0][:, :], soft_col[5][:, :], best[1][:, :], ALU.subtract)\
                    .then_inc(s["soft_d"], 1)

            def router_rows(n):
                link = chain(dve, "soft_step", n * 10)
                dve.wait_ge(s["soft_e"], n + 1)
                link(V.tensor_scalar(soft_col[2][:, :], soft_col[1][:, :], 1.0, 1e-12, ALU.add, ALU.max))
                link(V.reciprocal(soft_col[3][:, :], soft_col[2][:, :]))
                link(V.tensor_tensor(soft_col[2][:, :], soft_col[1][:, :], soft_col[3][:, :], ALU.mult))
                link(V.tensor_tensor(soft[0][:, :, :], first[1][:, :, :], wide(soft_col[3][:, :], 2, E), ALU.mult))
                link(V.tensor_tensor(soft[1][:, :, :], second[1][:, :, :], wide(soft_col[2][:, :], 2, E), ALU.mult))
                link(V.tensor_tensor(soft[2][:, :, :], soft[0][:, :, :], soft[1][:, :, :], ALU.add))
                after(dve, "rows_ps1", n)
                link(V.tensor_copy(rows[1][:, :, 0:E], soft[2][:, :, :]))
                link(V.tensor_tensor(soft[3][:, :, :], soft[2][:, :, :], rows[1][:, :, 0:E], ALU.subtract))
                link(V.tensor_copy(rows[1][:, :, E:2 * E], soft[3][:, :, :]))
                link(V.tensor_tensor(soft[4][:, :, :], soft[3][:, :, :], rows[1][:, :, E:2 * E], ALU.subtract))
                V.tensor_copy(rows[1][:, :, 2 * E:3 * E], soft[4][:, :, :]).then_inc(s["rows_done1"], 1)

            def x1_add(n):
                dve.wait_ge(s["x1_ps"], n + 1)
                dve.wait_ge(s["x_b2_done"], n + 1)
                after(dve, "x1_done", n)
                V.tensor_tensor(x1_new[:, :, :].rearrange("p b d -> p (b d)"), pa[:, :],
                                x_b2[:, :, :].rearrange("p b d -> p (b d)"), ALU.add).then_inc(s["x1_new_done"], 1)

            def x2_add(n):
                dve.wait_ge(s["y0_back"], n + 1)
                dve.wait_ge(s["x1_done"], n + 1)
                V.tensor_tensor(x2[:, :, :].rearrange("p b d -> p (b d)"), pa[:, :],
                                x1[:, :, :].rearrange("p b d -> p (b d)"), ALU.add).then_inc(s["x2_done"], 1)

            def x3_add(n):
                dve.wait_ge(s["fuse_ps"], n + 1)
                after(dve, "x3_tokens_done", n)
                V.tensor_tensor(x3[:, :, :].rearrange("p b d -> p (b d)"), pb[:, :],
                                x2[:, :, :].rearrange("p b d -> p (b d)"), ALU.add).then_inc(s["x3_done"], 1)

            def out_add(n):
                dve.wait_ge(s["y1_back"], n + 1)
                dve.wait_ge(s["x3_tokens_done"], n + 1)
                after(dve, "out_stored", n * 16)
                V.tensor_tensor(x_out[:, :, :].rearrange("p b d -> p (b d)"), pa[:, :],
                                x3_tokens[:, :, :].rearrange("p b d -> p (b d)"), ALU.add).then_inc(s["out_done"], 1)

            def block_prepare(n):
                dve.wait_ge(s["block_loaded"], n * 16 + 16)
                V.tensor_tensor(block[:, :, :], block_in[:, :, :], wide(ident[:, :], 1, 2), ALU.add)\
                    .then_inc(s["block_eye"], 1)
                dve.wait_ge(s["block_eye"], n + 1)
                link = chain(dve, "deg_step", n * 3)
                link(V.tensor_reduce(degree[:, :], block[:, :, :], AX, ALU.add))
                link(V.tensor_scalar(no_degree[:, :], degree[:, :], 0.0, None, ALU.is_equal))
                V.tensor_tensor(safe_degree[:, :], degree[:, :], no_degree[:, :], ALU.add).then_inc(s["deg_step"], 1)

            def block_scale(n):
                dve.wait_ge(s["deg_pow"], n + 1)
                V.scalar_tensor_tensor(out=has_degree[:, :], in0=no_degree[:, :], scalar=-1.0, in1=raised[:, :],
                                       op0=ALU.mult, op1=ALU.mult).then_inc(s["dinv_done"], 1)
                dve.wait_ge(s["dinv_done"], n * 2 + 1)
                V.tensor_tensor(dinv[:, :], raised[:, :], has_degree[:, :], ALU.add).then_inc(s["dinv_done"], 1)
                dve.wait_ge(s["dinv_done"], n * 2 + 2)
                after(dve, "norm_ps", n)
                V.tensor_tensor(block_row[:, :, :], block[:, :, :], wide(dinv[:, :], 2, P), ALU.mult)\
                    .then_inc(s["block_row_done"], 1)

            def norm_evacuate(n):
                dve.wait_ge(s["norm_ps"], n + 1)
                after(dve, "conv_ps", n)
                V.tensor_tensor(norm_t[:, :, :], pa[:, 0:2 * P].rearrange("p (a n) -> p a n", a=2),
                                wide(dinv[:, :], 2, P), ALU.mult).then_inc(s["norm_t_done"], 1)

            def hid1_bias(n):
                dve.wait_ge(s["hid1_ps"], n + 1)
                after(dve, "hid1_done", n)
                for c in range(2):
                    V.tensor_tensor(hid1_b[:, c, :, 0:USED],
                                    pb[:, c * G * S:(c + 1) * G * S].rearrange("p (b n) -> p b n", b=G)[:, :, 0:USED],
                                    wide(g1_b1[:, c, 0:USED], 1, G), ALU.add).then_inc(s["hid1_b_done"], 1)

            def conv_bias(n):
                dve.wait_ge(s["conv_ps"], n + 1)
                after(dve, "conv_done", n)
                V.tensor_tensor(conv_b[:, :, :], pb[:, 0:2 * P].rearrange("p (a d) -> p a d", a=2),
                                wide(g1_b2[:, :], 1, 2), ALU.add).then_inc(s["conv_b_done"], 1)

            def split_lo(k):
                dve.wait_ge(s["w_hi_done"], k + 1)
                V.tensor_tensor(w_lo[:, k, :], stage[:, k % 2, :], w_hi[:, k, :].bitcast(F32), ALU.subtract)\
                    .then_inc(s["w_lo_done"], 1)

            def split_b2():
                link = chain(dve, "b2_step", 0)
                link(V.tensor_copy(b2_part[:, 0, :, :], e_b2[:, :, :]))
                link(V.tensor_tensor(b2_rest[:, :, :], e_b2[:, :, :], b2_part[:, 0, :, :], ALU.subtract))
                link(V.tensor_copy(b2_part[:, 1, :, :], b2_rest[:, :, :]))
                link(V.tensor_tensor(b2_rest2[:, :, :], b2_rest[:, :, :], b2_part[:, 1, :, :], ALU.subtract))
                link(V.tensor_copy(b2_part[:, 2, :, :], b2_rest2[:, :, :]))
                link(V.tensor_scalar(b2_mix[:, 0, :], b2_part[:, 0, 0, :], part_rows[:, 0:1], None, ALU.mult))
                link(V.scalar_tensor_tensor(out=b2_mix[:, 1, :], in0=b2_part[:, 1, 0, :], scalar=part_rows[:, 1:2],
                                            in1=b2_mix[:, 0, :], op0=ALU.mult, op1=ALU.add))
                V.scalar_tensor_tensor(out=e0_b2[:, :], in0=b2_part[:, 2, 0, :], scalar=part_rows[:, 2:3],
                                       in1=b2_mix[:, 1, :], op0=ALU.mult, op1=ALU.add).then_inc(s["e0_b2_done"], 1)

            def fuse_start():
                dve.wait_ge(s["late_loaded"], 16 * len(LATE))
                link = chain(dve, "fuse_step", 0)
                link(V.tensor_reduce(fw_col[0][:, :], fuse_w[:, :], AX, ALU.max))
                V.tensor_scalar(fw[1][:, :], fuse_w[:, :], fw_col[0][:, 0:1], None, ALU.subtract)\
                    .then_inc(s["fuse_d"], 1)

            def fuse_finish():
                dve.wait_ge(s["fuse_pow"], 1)
                link = chain(dve, "fuse_step", 1)
                link(V.tensor_reduce(fw_col[1][:, :], fw[2][:, :], AX, ALU.add))
                link(V.reciprocal(fw_col[2][:, :], fw_col[1][:, :]))
                link(V.scalar_tensor_tensor(out=fw[3][:, :], in0=fw[2][:, :], scalar=fw_col[2][:, 0:1],
                                            in1=slot_group[:, :], op0=ALU.mult, op1=ALU.mult))
                link(V.tensor_reduce(fw_col[3][:, :], fw[3][:, :], AX, ALU.add))
                V.tensor_scalar(fuse[:, :, :], slot_token[:, :, :], fw_col[3][:, 0:1], None, ALU.mult)\
                    .then_inc(s["fuse_done"], 1)

            def start():
                dve.wait_ge(s["x_loaded"], 16)
                norm_stats(0, 0, x_in)
                dve.wait_ge(s["small_loaded"], 16 * len(SMALL))
                V.tensor_scalar(eps_col[:, :], eps_col[:, :], 1.0, None, ALU.add).then_inc(s["eps_done"], 1)
                dve.wait_ge(s["eps_done"], 1)
                V.tensor_scalar(eye_eps[:, :, :], wide(ident[:, :], 1, G), eps_col[:, 0:1], None, ALU.mult)\
                    .then_inc(s["eye_eps_done"], 1)
                dve.wait_ge(s["gate_w_hi"], 1)
                V.tensor_tensor(gate_lo[:, :, :], gate_w[:, :, :], gate_hi[:, :, :].bitcast(F32), ALU.subtract)\
                    .then_inc(s["gate_w_lo"], 1)
                split_b2()
                split_lo(0)
                x1_add(0)
                dve.wait_ge(s["x1_new_done"], 1)
                norm_stats(1, 0, x1_new)
                split_lo(1)
                xt_rest(0, 0, pa)
                dve.wait_ge(s["consts_set"], 4)
                gate_rows(0)

            def early(i, c0, f0=True, q=True, pre=True, fin=True):
                n, m, r = i + 1, i + 3, early_ring(i)
                if fin:
                    weigh(c0 - 1, (r - 1) % RING, i * C1 + C1)
                    lo(c0 - 2, (r - 2) % RING)
                for t in range(C0):
                    if t == 1 and fin:
                        lo(c0 - 1, (r - 1) % RING)
                    if t > 0 and f0:
                        lo(c0 + t - 1, (r + t - 1) % RING)
                    if t == 0 and not q:
                        fuse_start()
                    if t == 2 and not q:
                        split_lo(2)
                        fuse_finish()
                    if t == 2 and q:
                        hid1_bias(n)
                    if t == 3 and pre:
                        dve.wait_ge(s["x_loaded"], m * 16 + 16)
                        norm_stats(0, m, x_in)
                    if t == 6 and fin:
                        out_add(i)
                    if t == 7 and q:
                        conv_bias(n)
                    if t == 9 and q:
                        x3_add(n)
                        dve.wait_ge(s["x3_done"], n + 1)
                        norm_stats(3, n, x3)
                    if t == 12 and pre:
                        x1_add(m)
                    if t == 12 and q:
                        xt_rest(1, n, pb)
                    if t == 12 and pre:
                        dve.wait_ge(s["x1_new_done"], m + 1)
                        norm_stats(1, m, x1_new)
                    if t == 13 and q:
                        router_choose(n)
                    if t == 15 and q:
                        router_rows(n)

            def late(i, c0, f1=True, pre=True, back=True):
                r = late_ring(i)
                for t in range(C1):
                    if t == 0 and back:
                        lo(c0 - 1, (r - 1) % RING)
                    if f1 and t > 0:
                        weigh(c0 + t - 1, (r + t - 1) % RING, i * C1 + t)
                    if f1 and t > 1:
                        lo(c0 + t - 2, (r + t - 2) % RING)
                    if t == 1 and pre:
                        xt_rest(0, i + 2, pa)
                    if t == 1 and back:
                        block_prepare(i + 1)
                    if t == 3 and pre:
                        gate_rows(i + 2)
                    if t == 4 and back:
                        block_scale(i + 1)
                    if t == 5 and back:
                        x2_add(i + 1)
                        dve.wait_ge(s["x2_done"], i + 2)
                        norm_stats(2, i + 1, x2)
                    if t == 6 and back:
                        norm_evacuate(i + 1)

            def end(i, c):
                r = late_ring(i)
                weigh(c - 1, (r + C1 - 1) % RING, i * C1 + C1)
                lo(c - 2, (r + C1 - 2) % RING)
                lo(c - 1, (r + C1 - 1) % RING)
                out_add(i)

            schedule(dve, late, early, start, end)

        @block_ctx.tensor
        def _(pe):
            mm = nc.tensor.matmul

            def three(dst, w_hi_, w_lo_, x_hi_, x_lo_, first_=True, last_=True):
                mm(dst, w_hi_, x_hi_, start=first_, stop=False)
                mm(dst, w_hi_, x_lo_, start=False, stop=False)
                return mm(dst, w_lo_, x_hi_, start=False, stop=last_)

            def expert_w(part, third, at):
                return part[:, third, at * P:(at + 1) * P]

            def z0(c, ring, t, n):
                if t == 0:
                    pe.wait_ge(s["xt_lo0"], n + 1)
                    pe.wait_ge(s["rows_t0"], n + 1)
                after(pe, "gelu_done", c - Z_RING + 1)
                three(z[ring % Z_RING][:, :], expert_w(w_hi, 0, t), expert_w(w_lo, 0, t), xt_hi[0][:, :], xt_lo[0][:, :],
                      last_=False)
                mm(z[ring % Z_RING][:, :], shut[:, t // 2, :], rows_t[0][:, :], start=False, stop=True)\
                    .then_inc(s["z_ready"], 1)

            def y_0(c, ring, t, n):
                if t == 0:
                    after(pe, "y0_t", n)
                pe.wait_ge(s["lo_done"], c + 1)
                if t == C0 - 1:
                    mm(y0[:, :], e0_b2[:, :], rows_t[0][:, :], start=False, stop=False)
                last = three(y0[:, :], expert_w(w_hi, 1, t), expert_w(w_lo, 1, t), h_hi[:, ring, :], h_lo[:, ring, :],
                             first_=(t == 0), last_=(t == C0 - 1))
                last.then_inc(s["y_done"], 1)

            def z1(c, ring, t, n):
                if t == 0:
                    pe.wait_ge(s["xt_lo1"], n + 1)
                after(pe, "gelu_done", c - Z_RING + 1)
                three(z[ring % Z_RING][:, :], expert_w(w_hi, 2, t), expert_w(w_lo, 2, t), xt_hi[1][:, :], xt_lo[1][:, :])\
                    .then_inc(s["z_ready"], 1)

            def spread1(t, n):
                if t == 0:
                    pe.wait_ge(s["rows_t1"], n + 1)
                after(pe, "weighted_done", n * C1 + t)
                mm(spread[:, :], pick[:, t, :], rows_t[1][:, :], start=True, stop=True).then_inc(s["spread_ready"], 1)

            def y_1(c, ring, t, n):
                if t == 0:
                    after(pe, "y1_t", n)
                pe.wait_ge(s["lo_done"], c + 1)
                if t == C1 - 1:
                    for k in range(PARTS):
                        mm(y1[:, :], b2_part[:, k, 1, :], rows_t[1][:, :], start=False, stop=False)
                last = three(y1[:, :], expert_w(w_hi, 2, C1 + t), expert_w(w_lo, 2, C1 + t), h_hi[:, ring, :],
                             h_lo[:, ring, :], first_=(t == 0), last_=(t == C1 - 1))
                last.then_inc(s["y_done"], 1)

            def turn4(ps, src, name):
                for b in range(G):
                    last = nc.tensor.transpose(ps[:, b * P:(b + 1) * P], src(b), ident[:, :])
                last.then_inc(s[name], 1)

            def agg0_mm(n):
                pe.wait_ge(ln[0]["normed"], n * G + G)
                pe.wait_ge(s["adj_done"], n + 1)
                for b in range(G):
                    last = mm(pa[:, b * P:(b + 1) * P], normed[0][:, b, :], adj_eye[:, b, :], start=True, stop=True)
                last.then_inc(s["agg0_ps"], 1)

            def hid0_mm(n, c):
                if c == 0:
                    pe.wait_ge(s["agg0_done"], n + 1)
                else:
                    pe.wait_ge(s["hid0_done"], n * 2 + 1)
                mm(pa[:, :], g0_w1[:, c * P:(c + 1) * P], agg0[:, :], start=True, stop=True).then_inc(s["hid0_ps"], 1)

            def x1_mm(n):
                pe.wait_ge(s["hid0_done"], n * 2 + 2)
                for b in range(G):
                    for c in range(2):
                        last = mm(pa[:, b * P:(b + 1) * P], hid0[:, c, b * P:(b + 1) * P], g0_w2[:, c, :],
                                  start=(c == 0), stop=(c == 1))
                last.then_inc(s["x1_ps"], 1)

            def xt_mm(k, n, ps):
                pe.wait_ge(ln[3 if k else 1]["normed"], n * G + G)
                turn4(ps, lambda b: normed[3 if k else 1][:, b, :], f"xt_ps{k}")

            def score_mm(k, n, ps):
                pe.wait_ge(s[f"xt_lo{k}"], n + 1)
                for b in range(G):
                    dst, at = ps[:, b * E:(b + 1) * E], slice(b * P, (b + 1) * P)
                    mm(dst, xt_hi[k][:, at], gate_hi[:, k, :], start=True, stop=False)
                    mm(dst, xt_lo[k][:, at], gate_hi[:, k, :], start=False, stop=False)
                    last = mm(dst, xt_hi[k][:, at], gate_lo[:, k, :], start=False, stop=True)
                last.then_inc(s[f"score_ps{k}"], 1)

            def rows_mm(k, n):
                pe.wait_ge(s[f"rows_done{k}"], n + 1)
                for b in range(G):
                    last = nc.tensor.transpose(pb[:, :].bitcast(BF16)[:, b * P:(b + 1) * P], rows[k][:, b, :],
                                               identb[:, :])
                last.then_inc(s[f"rows_ps{k}"], 1)

            def y_back(k, n):
                pe.wait_ge(s[f"y{k}_t"], n + 1)
                src = y1_t if k else y0_t
                turn4(pa, lambda b: src[:, b * P:(b + 1) * P], f"y{k}_back")

            def norm_mm(n):
                pe.wait_ge(s["block_row_done"], n + 1)
                for p in range(2):
                    last = nc.tensor.transpose(pa[:, p * P:(p + 1) * P], block_row[:, p, :], ident[:, :])
                last.then_inc(s["norm_ps"], 1)

            def tok_mm(n):
                pe.wait_ge(s["norm_t_done"], n + 1)
                for p in range(2):
                    last = mm(pb[:, p * P:(p + 1) * P].rearrange("t (a n) -> t a n", a=2), slot_token[:, p, :],
                              norm_t[:, :, p * S:(p + 1) * S], start=True, stop=True)
                last.then_inc(s["tok_ps"], 1)

            def agg1_mm(n):
                pe.wait_ge(ln[2]["normed"], n * G + G)
                pe.wait_ge(s["norm_tok_done"], n + 1)
                for b in range(G):
                    last = mm(pa[:, b * S:(b + 1) * S], normed[2][:, b, :], norm_tok[:, b % 2, b // 2, :],
                              start=True, stop=True)
                last.then_inc(s["agg1_ps"], 1)

            def hid1_mm(n):
                pe.wait_ge(s["agg1_done"], n + 1)
                for c in range(2):
                    ps = pb[:, c * G * S:(c + 1) * G * S].rearrange("p (b n) -> p b n", b=G)
                    for g, nodes in enumerate(NODES):
                        at = slice(FIRST[g], FIRST[g] + len(nodes))
                        last = mm(ps[:, :, at], g1_w1[:, g, c, :], agg1[:, :, at], start=True, stop=True)
                last.then_inc(s["hid1_ps"], 1)

            def supp_t_mm(n):
                pe.wait_ge(s["hid1_done"], n + 1)
                ps = pb[:, 0:G * S].rearrange("p (b n) -> p b n", b=G)
                for g, nodes in enumerate(NODES):
                    at = slice(FIRST[g], FIRST[g] + len(nodes))
                    for c in range(2):
                        last = mm(ps[:, :, at], g1_w2[:, g, c, :], hid1[:, c, :, at], start=(c == 0), stop=(c == 1))
                last.then_inc(s["supp_t_ps"], 1)

            def supp_mm(n):
                pe.wait_ge(s["supp_t_done"], n + 1)
                for p in range(2):
                    last = nc.tensor.transpose(pb[:, p * P:(p + 1) * P],
                                               supp_t[:, 2 * p:2 * p + 2, :].rearrange("d b n -> d (b n)"),
                                               ident[:, :])
                last.then_inc(s["supp_ps"], 1)

            def conv_mm(n):
                pe.wait_ge(s["supp_done"], n + 1)
                for p in range(2):
                    last = mm(pb[:, p * P:(p + 1) * P], norm_t[:, p, :], supp[:, p, :], start=True, stop=True)
                last.then_inc(s["conv_ps"], 1)

            def fuse_mm(n):
                pe.wait_ge(s["conv_done"], n + 1)
                for b in range(G):
                    last = mm(pb[:, b * P:(b + 1) * P], fuse[:, b % 2, :], conv[:, b // 2, :], start=True, stop=True)
                last.then_inc(s["fuse_ps"], 1)

            def start():
                pe.wait_ge(s["small_loaded"], 16 * len(SMALL))
                agg0_mm(0)
                hid0_mm(0, 0)
                hid0_mm(0, 1)
                x1_mm(0)
                xt_mm(0, 0, pa)
                pe.wait_ge(s["gate_w_lo"], 1)
                score_mm(0, 0, pb)
                pe.wait_ge(s["bf16_consts"], 3)
                rows_mm(0, 0)
                pe.wait_ge(s["w_lo_done"], 2)
                pe.wait_ge(s["e0_b2_done"], 1)

            def early(i, c0, f0=True, q=True, pre=True, fin=True):
                n, m, r = i + 1, i + 3, early_ring(i)
                for t in range(C0):
                    if f0:
                        z0(c0 + t, (r + t) % RING, t, i + 2)
                    if t < LAG and fin:
                        y_1(c0 + t - LAG, (r + t - LAG) % RING, C1 + t - LAG, i)
                    if t >= LAG and f0:
                        y_0(c0 + t - LAG, (r + t - LAG) % RING, t - LAG, i + 2)
                    if t == 0 and fin:
                        spread1(C1 - 1, i)
                    if t == 1 and q:
                        pe.wait_ge(s["norm_t_done"], n + 1)
                        agg1_mm(n)
                    if t == 2 and q:
                        pe.wait_ge(s["norm_tok_done"], n + 1)
                        if not fin:
                            pe.wait_ge(s["late_loaded"], 16 * len(LATE))
                        hid1_mm(n)
                    if t == 4 and q:
                        pe.wait_ge(s["hid1_b_done"], n * 2 + 2)
                        supp_t_mm(n)
                    if t == 5 and fin:
                        pe.wait_ge(s["agg1_done"], n + 1)
                        y_back(1, i)
                    if t == 5 and q:
                        supp_mm(n)
                    if t == 6 and pre:
                        after(pe, "out_done", i + 1)
                        if not q:
                            pe.wait_ge(s["xt_lo0"], 1)
                        agg0_mm(m)
                    if t == 7 and q:
                        conv_mm(n)
                    if t == 8 and pre:
                        hid0_mm(m, 0)
                    if t == 9 and q:
                        pe.wait_ge(s["conv_b_done"], n + 1)
                        if not fin:
                            pe.wait_ge(s["fuse_done"], 1)
                        fuse_mm(n)
                    if t == 10 and pre:
                        hid0_mm(m, 1)
                    if t == 11 and pre:
                        x1_mm(m)
                    if t == 12 and q:
                        pe.wait_ge(s["x3_done"], n + 1)
                        xt_mm(1, n, pb)
                    if t == 13 and q:
                        if pre:
                            pe.wait_ge(s["x1_new_done"], m + 1)
                        else:
                            pe.wait_ge(s["out_done"], i + 1)
                        score_mm(1, n, pa)
                if q and not fin:
                    pe.wait_ge(s["w_lo_done"], 3)

            def late(i, c0, f1=True, pre=True, back=True):
                r = late_ring(i)
                for t in range(C1):
                    if f1:
                        z1(c0 + t, (r + t) % RING, t, i)
                    if t < LAG and back:
                        y_0(c0 + t - LAG, (r + t - LAG) % RING, C0 + t - LAG, i + 1)
                    if t >= LAG and f1:
                        y_1(c0 + t - LAG, (r + t - LAG) % RING, t - LAG, i)
                    if t == 0 and f1:
                        pe.wait_ge(s["xt_lo1"], i + 1)
                        rows_mm(1, i)
                    if t > 0 and f1:
                        spread1(t - 1, i)
                    if t == 1 and pre:
                        after(pe, "score_done1", i + 1)
                        xt_mm(0, i + 2, pa)
                    if t == 2 and pre:
                        after(pe, "rows_t1", i + 1)
                        score_mm(0, i + 2, pb)
                    if t == 5 and back:
                        if pre:
                            pe.wait_ge(s["xt_lo0"], i + 3)
                        else:
                            pe.wait_ge(s["score_done1"], i + 1)
                        y_back(0, i + 1)
                    if t == 6 and pre:
                        pe.wait_ge(s["score_done0"], i + 3)
                        rows_mm(0, i + 2)
                    if t == 6 and back:
                        pe.wait_ge(s["x2_done"], i + 2)
                        norm_mm(i + 1)
                    if t == 7 and back:
                        if pre:
                            pe.wait_ge(s["rows_t0"], i + 3)
                        else:
                            pe.wait_ge(s["rows_t1"], i + 1)
                        tok_mm(i + 1)

            def end(i, c):
                r = late_ring(i)
                spread1(C1 - 1, i)
                for t in range(C1 - LAG, C1):
                    y_1(c - C1 + t, (r + t) % RING, t, i)
                y_back(1, i)

            schedule(pe, late, early, start, end)


def constants():
    import numpy as np

    ident = np.eye(P, dtype=np.float32)
    far = 2.0 ** 100
    shut = np.zeros((P, E), np.float32)
    pick = np.zeros((P, E), np.float32)
    for e in range(E):
        shut[e, e] = far
        shut[ONES, e] = -far
        for k in range(PARTS):
            pick[k * E + e, e] = 1
    part_rows = np.zeros((P, PARTS), np.float32)
    for k in range(PARTS):
        part_rows[k * E:(k + 1) * E, k] = 1
    slot_token = np.zeros((P, 2, P), np.float32)
    slot_group = np.zeros((P, 5), np.float32)
    for g, nodes in enumerate(NODES):
        for k, token in enumerate(nodes):
            for p in range(2):
                slot_token[p * S + FIRST[g] + k, p, token] = 1
                slot_group[p * S + FIRST[g] + k, g] = 1
    return {"ident": ident,
            "rank": np.tile(np.arange(E, 0, -1, dtype=np.float32), (P, 1)),
            "shut_rows": shut, "pick_rows": pick,
            "part_rows": part_rows, "slot_token": slot_token, "slot_group": slot_group}


def layout(v):
    import numpy as np

    def rows(name):
        return np.broadcast_to(v[name].reshape(1, -1), (P, v[name].size))

    adj = v["adj"]
    block = np.zeros((P, PAIRS, P), adj.dtype)
    slot_b1 = np.zeros((P, 2, S), adj.dtype)
    slot_b2 = np.zeros((P, P), adj.dtype)
    for g, nodes in enumerate(NODES):
        for k, token in enumerate(nodes):
            slot_b1[:, :, FIRST[g] + k] = v["L1_gnn_b1"][g].reshape(2, P).T
            for p in range(2):
                slot = p * S + FIRST[g]
                block[slot + k, :, slot:slot + len(nodes)] = adj[p::2, token][:, nodes]
                slot_b2[slot + k] = v["L1_gnn_b2"][g]
    e_b2 = np.zeros((P, 2, P), adj.dtype)
    for k in range(PARTS):
        e_b2[k * E:(k + 1) * E, 0] = v["L0_ffn_b2"]
        e_b2[k * E:(k + 1) * E, 1] = v["L1_ffn_b2"]
    w1 = v["L1_ffn_w1"].transpose(1, 0, 2).reshape(P, E * P)
    w2 = v["L1_ffn_w2"].transpose(1, 0, 2).reshape(P, E * P)
    return {
        "x": v["x"].transpose(1, 0, 2),
        "adj": adj.transpose(2, 0, 1),
        "block": block,
        "eps": rows("L0_gnn_eps"),
        "g0_w1": v["L0_gnn_W1"],
        "g0_w2": v["L0_gnn_W2"].reshape(2, P, P).transpose(1, 0, 2),
        "g0_b1": v["L0_gnn_b1"].reshape(2, P).T,
        "g0_b2": rows("L0_gnn_b2"),
        "gate_w": np.stack([v["L0_ffn_Wg"], v["L1_ffn_router_w"].T], axis=1),
        "gate_b": rows("L0_ffn_bg"),
        "e0_w1": v["L0_ffn_W1"].transpose(1, 0, 2).reshape(P, C0 * P),
        "e0_w2": v["L0_ffn_W2"].reshape(E, 2, P, P).transpose(2, 0, 1, 3).reshape(P, C0 * P),
        "e0_b1": v["L0_ffn_b1"].reshape(C0, P).T,
        "e1_w": np.concatenate([w1, w2], axis=1),
        "e1_b1": v["L1_ffn_b1"].T,
        "e_b2": e_b2,
        "g1_w1": v["L1_gnn_W1"].reshape(5, P, 2, P).transpose(1, 0, 2, 3),
        "g1_w2": v["L1_gnn_W2"].reshape(5, 2, P, P).transpose(2, 0, 1, 3),
        "g1_b1": slot_b1,
        "g1_b2": slot_b2,
        "fuse_w": rows("L1_gnn_fusion_w"),
    }


def kernel(**inputs):
    import concourse.bacc as bacc
    import numpy as np
    from concourse.bass_utils import run_bass_kernel_spmd

    nc = bacc.Bacc("TRN2", target_bir_lowering=False, num_devices=1)
    arrays, args = {}, {}
    values = {name: np.asarray(value) for name, value in inputs.items()}
    for name, value in {**layout(values), **constants()}.items():
        value = np.ascontiguousarray(value)
        arrays[f"in_{name}"] = value
        args[name] = nc.dram_tensor(f"in_{name}", value.shape, mybir.dt.from_np(value.dtype),
                                    kind="ExternalInput").ap()
    out = nc.dram_tensor("out_x", (P, B, P), F32, kind="ExternalOutput").ap()
    program(nc, args, out)
    result = run_bass_kernel_spmd(nc, [arrays], core_ids=[0]).results[0]["out_x"]
    return np.ascontiguousarray(result.transpose(1, 0, 2))
```

```python
from contextlib import ExitStack

import concourse.bass as bass
from concourse import mybir

F32 = mybir.dt.float32
F32R = mybir.dt.float32r
BF16 = mybir.dt.bfloat16
ALU = mybir.AluOpType
ACT = mybir.ActivationFunctionType
AX = mybir.AxisListType.X

P = 128
B = 64
G = 4
T = G * P
GROUPS = B // G
E = 8
C0 = 16
C1 = 8
Z_RING = 3
RING = 6
LAG = 4
POOL_LO = (2,)
PARTS = 3
ONES = PARTS * E
NODES = [list(range(25)), [0, 1, 2, 3, 4, 5, 6, 7, 8], [0, 9, 10, 11, 12, 13, 14], [6, 7, 8, 12, 13, 14],
         [3, 4, 5, 9, 10, 11]]
FIRST = [sum(len(n) for n in NODES[:k]) for k in range(len(NODES))]
USED = sum(len(n) for n in NODES)
S = 64
PAIRS = B // 2
EPS = 1e-5

SMALL = {"ident": (P,), "eps": (1,), "g0_w1": (2 * P,), "g0_w2": (2, P), "g0_b1": (2,), "g0_b2": (P,),
         "gate_w": (2, E), "gate_b": (E,), "rank": (E,), "shut_rows": (E,), "pick_rows": (E,), "e0_b1": (C0,),
         "e_b2": (2, P), "part_rows": (PARTS,)}
LATE = {"fuse_w": (5,), "slot_group": (5,), "slot_token": (2, P), "g1_w1": (5, 2, P), "g1_w2": (5, 2, P),
        "g1_b1": (2, S), "g1_b2": (P,), "e1_b1": (C1,)}


def size(shape):
    n = 1
    for d in shape:
        n = n * d
    return n


def program(nc, a, out):
    ctx = ExitStack()
    with ctx:
        def sb(name, shape, dt=F32):
            return ctx.enter_context(nc.sbuf_tensor(name, shape, dt))

        def psum(name):
            return ctx.enter_context(nc.psum_tensor(name, [P, T], F32))

        def sem(name):
            return ctx.enter_context(nc.semaphore(name))

        def views(tile, fields):
            at, found = 0, {}
            for name, shape in fields.items():
                view = tile[:, at:at + size(shape)]
                if len(shape) == 2:
                    view = view.rearrange("p (a b) -> p a b", a=shape[0])
                if len(shape) == 3:
                    view = view.rearrange("p (a b c) -> p a b c", a=shape[0], b=shape[1])
                found[name] = view
                at += size(shape)
            return found

        small = sb("small", [P, sum(size(shape) for shape in SMALL.values())])
        late_in = sb("late_in", [P, sum(size(shape) for shape in LATE.values())])
        v = {**views(small, SMALL), **views(late_in, LATE)}
        ident, g0_w1, g0_w2, g0_b1, g0_b2 = (v[n] for n in ("ident", "g0_w1", "g0_w2", "g0_b1", "g0_b2"))
        gate_w, gate_b, rank, eps_in = (v[n] for n in ("gate_w", "gate_b", "rank", "eps"))
        shut_rows, pick_rows, part_rows = (v[n] for n in ("shut_rows", "pick_rows", "part_rows"))
        e0_b1, e1_b1, e_b2 = (v[n] for n in ("e0_b1", "e1_b1", "e_b2"))
        fuse_w, slot_group, slot_token = (v[n] for n in ("fuse_w", "slot_group", "slot_token"))
        g1_w1, g1_w2, g1_b1, g1_b2 = (v[n] for n in ("g1_w1", "g1_w2", "g1_b1", "g1_b2"))
        identb = sb("identb", [P, P], BF16)
        eye_eps = sb("eye_eps", [P, G, P])
        eps_col = sb("eps_col", [P, 1])
        pow_half = sb("pow_half", [P, G])
        table_warm = sb("table_warm", [P, G])
        pow_base = sb("pow_base", [P, G * E])
        gate_part = sb("gate_part", [P, 2, 2, E], F32R)
        stage = sb("stage", [P, 2, 2048])
        w_hi = sb("w_hi", [P, 3, 2048], F32R)
        w_lo = sb("w_lo", [P, 3, 2048], F32R)
        b2_rest = sb("b2_rest", [P, 2, P])
        b2_rest2 = sb("b2_rest2", [P, 2, P])
        b2_part = sb("b2_part", [P, PARTS, 2, P], BF16)
        b2_mix = sb("b2_mix", [P, PARTS, P])
        e0_b2 = sb("e0_b2", [P, P], BF16)
        shut = sb("shut", [P, E, P], BF16)
        pick = sb("pick", [P, E, P], BF16)
        fuse = sb("fuse", [P, 2, P])
        fw = [sb(f"fw{n}", [P, 5]) for n in range(4)]
        fw_col = [sb(f"fw_col{n}", [P, 1]) for n in range(4)]

        x_in = sb("x_in", [P, G, P])
        adj_in = sb("adj_in", [P, G, P])
        adj_eye = sb("adj_eye", [P, G, P])
        x_b2 = sb("x_b2", [P, G, P])
        agg0 = sb("agg0", [P, T])
        hid0 = sb("hid0", [P, 2, T])
        x1_new = sb("x1_new", [P, G, P])
        x1 = sb("x1", [P, G, P])
        stats = [sb(f"stats{n}", [P, G, 6]) for n in range(4)]
        mean_var = [sb(f"mean_var{n}", [P, G, 2]) for n in range(4)]
        var_eps = [sb(f"var_eps{n}", [P, G]) for n in range(4)]
        minus_mean = [sb(f"minus_mean{n}", [P, G]) for n in range(4)]
        shift = [sb(f"shift{n}", [P, G]) for n in range(4)]
        rstd = [sb(f"rstd{n}", [P, G]) for n in range(4)]
        normed = [sb(f"normed{n}", [P, G, P]) for n in range(4)]
        xt_hi = [sb(f"xt_hi{n}", [P, T], F32R) for n in range(2)]
        xt_lo = [sb(f"xt_lo{n}", [P, T], F32R) for n in range(2)]
        score = [sb(f"score{n}", [P, G, E]) for n in range(2)]
        score_b = sb("score_b", [P, G, E])
        sorted_scores = [sb(f"sorted_scores{n}", [P, G, E]) for n in range(2)]
        reaches = [sb(f"reaches{n}", [P, G, E]) for n in range(2)]
        exceeds = [sb(f"exceeds{n}", [P, G, E]) for n in range(2)]
        ranked = [sb(f"ranked{n}", [P, G, E]) for n in range(2)]
        order = [sb(f"order{n}", [P, G, E]) for n in range(2)]
        sorted_order = [sb(f"sorted_order{n}", [P, G, E]) for n in range(2)]
        exponent = sb("exponent", [P, G])
        power = sb("power", [P, G])
        chosen = sb("chosen", [P, G, E])
        first = sb("first", [P, G, E])
        second = sb("second", [P, G, E])
        picked = sb("picked", [P, G, E])
        total = sb("total", [P, G])
        per_total = sb("per_total", [P, G])
        weight = sb("weight", [P, G, E])
        weight_rest = sb("weight_rest", [P, G, E])
        weight_rest2 = sb("weight_rest2", [P, G, E])
        rows = [sb(f"rows{n}", [P, G, P], BF16) for n in range(2)]
        rows_t = [sb(f"rows_t{n}", [P, T], BF16) for n in range(2)]
        hid = sb("hid", [P, RING, T])
        h_hi = sb("h_hi", [P, RING, T], F32R)
        h_lo = sb("h_lo", [P, RING, T], F32R)
        y0_t = sb("y0_t", [P, T])
        y1_t = sb("y1_t", [P, T])
        x2 = sb("x2", [P, G, P])
        x3 = sb("x3", [P, G, P])
        x3_tokens = sb("x3_tokens", [P, G, P])
        x_out = sb("x_out", [P, G, P])
        block_in = sb("block_in", [P, 2, P])
        block = sb("block", [P, 2, P])
        degree = sb("degree", [P, 2])
        no_degree = sb("no_degree", [P, 2])
        safe_degree = sb("safe_degree", [P, 2])
        raised = sb("raised", [P, 2])
        has_degree = sb("has_degree", [P, 2])
        dinv = sb("dinv", [P, 2])
        block_row = sb("block_row", [P, 2, P])
        norm_t = sb("norm_t", [P, 2, P])
        norm_tok = sb("norm_tok", [P, 2, 2, S])
        agg1 = sb("agg1", [P, G, S])
        hid1_b = sb("hid1_b", [P, 2, G, S])
        hid1 = sb("hid1", [P, 2, G, S])
        supp_t = sb("supp_t", [P, G, S])
        supp = sb("supp", [P, 2, P])
        conv_b = sb("conv_b", [P, 2, P])
        conv = sb("conv", [P, 2, P])

        z = [psum(f"z{n}") for n in range(Z_RING)]
        y0 = psum("y0")
        y1 = psum("y1")
        spread = psum("spread")
        pa = psum("pa")
        pb = psum("pb")

        def spread_bank(t):
            return {1: y1, 3: y0, 5: y0, 7: y0}.get(t, spread)

        names = """x_loaded adj_loaded block_loaded small_loaded late_loaded bf16_consts w_loaded0 w_loaded1 w_loaded2 w_hi_done w_lo_done
            consts_set pool_consts table_loaded gate_w_hi gate_w_lo eye_eps_done eps_done b2_step e0_b2_done
            fuse_step fuse_d fuse_pow fuse_done
            adj_done x_b2_done agg0_ps agg0_done hid0_ps hid0_done x1_ps x1_new_done x1_done
            xt_ps0 xt_ps1 xt_hi0 xt_hi1 xt_lo0 xt_lo1 score_ps0 score_ps1 score_done0 score_done1 score_b_done
            pick_step0 pick_step1 chosen_done soft_d soft_e soft_step
            rows_done0 rows_done1 rows_ps0 rows_ps1 rows_t0 rows_t1
            z_ready gelu_done hi_done lo_done y_done spread_ready weighted_done
            y0_t y0_back x2_done y1_t y1_back out_done out_stored
            block_eye deg_step deg_pow dinv_done block_row_done norm_ps norm_t_done tok_ps norm_tok_done
            agg1_ps agg1_done hid1_ps hid1_b_done hid1_done supp_t_ps supp_t_done supp_ps supp_done
            conv_ps conv_b_done conv_done fuse_ps x3_done x3_tokens_done dve_held pool_held sp_held""".split()
        s = {n: sem(n) for n in names}
        ln = [{k: sem(f"ln{n}_{k}") for k in ("stats", "moments", "var", "minus", "rstd", "shift", "normed")} for n in range(4)]

        def after(eng, name, value):
            if not (isinstance(value, int) and value <= 0):
                eng.wait_ge(s[name], value)

        def wide(ap, dim, n):
            return ap.unsqueeze(dim).to_broadcast([*ap.shape[:dim], n, *ap.shape[dim:]])

        def chain(eng, name, base):
            done = [base]

            def link(ins, wait=True):
                done[0] = done[0] + 1
                ins.then_inc(s[name], 1)
                if wait:
                    eng.wait_ge(s[name], done[0])
            return link

        block_ctx = ctx.enter_context(nc.Block())

        def schedule(eng, late, early, start, end):
            turn = C0 + C1
            start()
            early(-2, 0, q=False, fin=False)
            late(-1, C0, f1=False)
            early(-1, C0, fin=False)
            late(0, 2 * C0)
            early(0, 2 * C0 + C1)
            with eng.Fori(1, GROUPS - 3) as i:
                late(i, i * turn + 2 * C0)
                early(i, i * turn + 2 * C0 + C1)
            i = GROUPS - 3
            late(i, i * turn + 2 * C0)
            early(i, i * turn + 2 * C0 + C1, pre=False)
            i = GROUPS - 2
            late(i, i * turn + 2 * C0, pre=False)
            early(i, i * turn + 2 * C0 + C1, f0=False, pre=False)
            late(i + 1, i * turn + 2 * C0 + C1, pre=False, back=False)
            end(i + 1, i * turn + 2 * C0 + 2 * C1)

        assert (C0 + C1) % RING == 0 and RING % Z_RING == 0 and LAG + 2 <= RING

        def late_ring(i):
            return {-1: C0, GROUPS - 1: 2 * C0 + C1}.get(i if isinstance(i, int) else 0, 2 * C0) % RING

        def early_ring(i):
            return {-2: 0, -1: C0}.get(i if isinstance(i, int) else 0, 2 * C0 + C1) % RING

        @block_ctx.sync
        def _(sp):
            def held():
                sp.sem_inc(s["sp_held"], 1)

            def load_x(n):
                after(sp, "x_b2_done", n)
                held()
                if not (isinstance(n, int) and n == 0):
                    sp.wait_ge(ln[0]["normed"], n * G)
                held()
                sp.dma_start(x_in[:, :, :], a["x"][:, bass.ds(n * G, G), :]).then_inc(s["x_loaded"], 16)
                after(sp, "adj_done", n)
                held()
                sp.dma_start(adj_in[:, :, :], a["adj"][:, bass.ds(n * G, G), :]).then_inc(s["adj_loaded"], 16)

            def load_block(n):
                after(sp, "block_eye", n)
                held()
                sp.dma_start(block_in[:, :, :], a["block"][:, bass.ds(n * 2, 2), :]).then_inc(s["block_loaded"], 16)

            load_x(0)
            sp.dma_start(stage[:, 0, :], a["e0_w1"]).then_inc(s["w_loaded0"], 16)
            sp.dma_start(stage[:, 1, :], a["e0_w2"]).then_inc(s["w_loaded1"], 16)
            load_block(0)
            load_x(1)
            sp.dma_start(late_in[:, :], a["late"]).then_inc(s["late_loaded"], 16)
            sp.wait_ge(s["w_lo_done"], 1)
            sp.dma_start(stage[:, 0, :], a["e1_w"]).then_inc(s["w_loaded2"], 16)
            load_x(2)
            with sp.Fori(3, GROUPS) as n:
                load_block(n - 2)
                load_x(n)
            load_block(GROUPS - 2)
            load_block(GROUPS - 1)

        @block_ctx.scalar
        def _(act):
            def copy(dst, src):
                return nc.scalar.activation(dst, src, ACT.Copy)

            def gelu(c, ring, bias):
                act.wait_ge(s["z_ready"], c + 1)
                after(act, "lo_done", c - RING + 1)
                nc.scalar.activation(hid[:, ring, :], z[ring % Z_RING][:, :], ACT.Gelu, bias=bias).then_inc(s["gelu_done"], 1)

            def agg0_copy(n):
                act.wait_ge(s["agg0_ps"], n + 1)
                after(act, "hid0_ps", n * 2)
                copy(agg0[:, :], pa[:, :]).then_inc(s["agg0_done"], 1)

            def relu0(n, c):
                act.wait_ge(s["hid0_ps"], n * 2 + c + 1)
                after(act, "x1_ps", n)
                nc.scalar.activation(hid0[:, c, :], pa[:, :], ACT.Relu, bias=g0_b1[:, c:c + 1])\
                    .then_inc(s["hid0_done"], 1)

            def keep_x1(n):
                act.wait_ge(s["x1_new_done"], n + 1)
                after(act, "x2_done", n)
                copy(x1[:, :, :], x1_new[:, :, :]).then_inc(s["x1_done"], 1)

            def xt_copy(k, n, ps):
                act.wait_ge(s[f"xt_ps{k}"], n + 1)
                after(act, f"score_ps{k}", n)
                copy(xt_hi[k][:, :], ps[:, :]).then_inc(s[f"xt_hi{k}"], 1)

            def rows_copy(k, n):
                act.wait_ge(s[f"rows_ps{k}"], n + 1)
                copy(rows_t[k][:, :], pb[:, :].bitcast(BF16)[:, 0:T]).then_inc(s[f"rows_t{k}"], 1)

            def y_copy(k, n, c):
                act.wait_ge(s["y_done"], c)
                after(act, f"y{k}_back", n)
                copy((y1_t if k else y0_t)[:, :], (y1 if k else y0)[:, :]).then_inc(s[f"y{k}_t"], 1)

            def norm_tok_copy(n):
                act.wait_ge(s["tok_ps"], n + 1)
                after(act, "agg1_ps", n)
                copy(norm_tok[:, :, :, :].rearrange("p a b c -> p (a b c)"), pb[:, 0:G * S])\
                    .then_inc(s["norm_tok_done"], 1)

            def agg1_copy(n):
                act.wait_ge(s["agg1_ps"], n + 1)
                after(act, "hid1_ps", n)
                copy(agg1[:, :, 0:USED], pa[:, 0:G * S].rearrange("p (b n) -> p b n", b=G)[:, :, 0:USED])\
                    .then_inc(s["agg1_done"], 1)

            def relu1(n):
                act.wait_ge(s["hid1_b_done"], n * 2 + 2)
                after(act, "supp_t_ps", n)
                nc.scalar.activation(hid1[:, :, :, 0:USED].rearrange("p c b n -> p (c b) n"),
                                     hid1_b[:, :, :, 0:USED].rearrange("p c b n -> p (c b) n"),
                                     ACT.Relu).then_inc(s["hid1_done"], 1)

            def supp_t_copy(n):
                act.wait_ge(s["supp_t_ps"], n + 1)
                after(act, "supp_ps", n)
                copy(supp_t[:, :, 0:USED], pb[:, 0:G * S].rearrange("p (b n) -> p b n", b=G)[:, :, 0:USED])\
                    .then_inc(s["supp_t_done"], 1)

            def supp_copy(n):
                act.wait_ge(s["supp_ps"], n + 1)
                after(act, "conv_ps", n)
                copy(supp[:, :, :].rearrange("p a d -> p (a d)"), pb[:, 0:2 * P]).then_inc(s["supp_done"], 1)

            def relu2(n):
                act.wait_ge(s["conv_b_done"], n + 1)
                after(act, "fuse_ps", n)
                nc.scalar.activation(conv[:, :, :], conv_b[:, :, :], ACT.Relu).then_inc(s["conv_done"], 1)

            def store(n):
                act.wait_ge(s["out_done"], n + 1)
                act.dma_start(out[:, bass.ds(n * G, G), :], x_out[:, :, :]).then_inc(s["out_stored"], 16)

            def split_hi(k):
                act.wait_ge(s[f"w_loaded{k}"], 16)
                copy(w_hi[:, k, :], stage[:, k % 2, :]).then_inc(s["w_hi_done"], 1)

            def norm_apply(k, n, src, used):
                act.wait_ge(ln[k]["shift"], n + 1)
                after(act, used, n)
                for b in range(G):
                    nc.scalar.activation(normed[k][:, b, :], src[:, b, :], ACT.Identity, bias=shift[k][:, b:b + 1],
                                         scale=rstd[k][:, b:b + 1]).then_inc(ln[k]["normed"], 1)

            def start():
                act.dma_start(small[:, :], a["small"]).then_inc(s["small_loaded"], 16)
                act.wait_ge(s["pool_consts"], 1)
                nc.scalar.activation(table_warm[:, :], pow_half[:, :], ACT.Gelu).then_inc(s["table_loaded"], 1)
                norm_apply(0, 0, x_in, "agg0_ps")
                act.wait_ge(s["small_loaded"], 16)
                copy(gate_part[:, :, 0, :], gate_w[:, :, :]).then_inc(s["gate_w_hi"], 1)
                copy(identb[:, :], ident[:, :]).then_inc(s["bf16_consts"], 1)
                agg0_copy(0)
                relu0(0, 0)
                relu0(0, 1)
                split_hi(0)
                copy(shut[:, :, :], wide(shut_rows[:, :], 2, P)).then_inc(s["bf16_consts"], 1)
                copy(pick[:, :, :], wide(pick_rows[:, :], 2, P)).then_inc(s["bf16_consts"], 1)
                norm_apply(1, 0, x1_new, "xt_ps0")
                xt_copy(0, 0, pa)
                split_hi(1)
                rows_copy(0, 0)

            def early(i, c0, f0=True, q=True, pre=True, fin=True):
                n, m, r = i + 1, i + 3, early_ring(i)
                for t in range(C0):
                    if t == LAG and fin:
                        y_copy(1, i, c0)
                    if f0:
                        gelu(c0 + t, (r + t) % RING, e0_b1[:, t:t + 1])
                    if t == 4 and not q:
                        act.wait_ge(s["late_loaded"], 16)
                        split_hi(2)
                    if t == 1 and q:
                        agg1_copy(n)
                    if t == 2 and q:
                        relu1(n)
                    if t == 4 and q:
                        supp_t_copy(n)
                    if t == 5 and q:
                        supp_copy(n)
                    if t == 4 and pre:
                        norm_apply(0, m, x_in, "agg0_ps")
                    if t == 6 and q:
                        relu2(n)
                    if t == 6 and pre:
                        agg0_copy(m)
                    if t == 8 and pre:
                        relu0(m, 0)
                    if t == 7 and f0:
                        keep_x1(i + 2)
                    if t == 8 and fin:
                        store(i)
                    if t == 9 and q:
                        norm_apply(3, n, x3, "xt_ps1")
                    if t == 10 and pre:
                        relu0(m, 1)
                    if t == 10 and q:
                        xt_copy(1, n, pb)

                    if t == 15 and pre:
                        norm_apply(1, m, x1_new, "xt_ps0")

            def late(i, c0, f1=True, pre=True, back=True):
                r = late_ring(i)
                for t in range(C1):
                    if t == LAG and back:
                        y_copy(0, i + 1, c0)
                    if t == 0 and f1:
                        rows_copy(1, i)
                    if f1:
                        gelu(c0 + t, (r + t) % RING, e1_b1[:, t:t + 1])
                    if t == 1 and pre:
                        xt_copy(0, i + 2, pa)
                    if t == 1 and back:
                        norm_tok_copy(i + 1)
                    if t == 5 and pre:
                        rows_copy(0, i + 2)
                    if t == 6 and back:
                        norm_apply(2, i + 1, x2, "agg1_ps")

            def end(i, c):
                y_copy(1, i, c)
                store(i)
                act.wait_ge(s["out_stored"], 16 * GROUPS)

            schedule(act, late, early, start, end)

        @block_ctx.gpsimd
        def _(pool):
            def held():
                pool.sem_inc(s["pool_held"], 1)

            def hi0(c, ring):
                pool.wait_ge(s["gelu_done"], c + 1)
                after(pool, "y_done", c - RING + 1)
                held()
                nc.gpsimd.tensor_scalar(h_hi[:, ring, :], hid[:, ring, :], 1.0, 0.0, ALU.mult, ALU.add)\
                    .then_inc(s["hi_done"], 1)

            def lo1(c, ring):
                pool.wait_ge(s["hi_done"], c + 1)
                nc.gpsimd.tensor_tensor(h_lo[:, ring, :], hid[:, ring, :], h_hi[:, ring, :].bitcast(F32), ALU.subtract)\
                    .then_inc(s["lo_done"], 1)

            def hi1(c, ring, done):
                pool.wait_ge(s["weighted_done"], done)
                after(pool, "y_done", c - RING + 1)
                held()
                nc.gpsimd.tensor_scalar(h_hi[:, ring, :], hid[:, ring, :], 1.0, 0.0, ALU.mult, ALU.add)\
                    .then_inc(s["hi_done"], 1)

            def rstd_pow(k, n):
                pool.wait_ge(ln[k]["var"], n + 1)
                if not (isinstance(n, int) and n == 0):
                    pool.wait_ge(ln[k]["normed"], n * G)
                nc.gpsimd.tensor_tensor(rstd[k][:, :], var_eps[k][:, :], pow_half[:, :], ALU.pow)\
                    .then_inc(ln[k]["rstd"], 1)
                pool.wait_ge(ln[k]["rstd"], n + 1)
                pool.wait_ge(ln[k]["minus"], n + 1)
                nc.gpsimd.tensor_tensor(shift[k][:, :], minus_mean[k][:, :], rstd[k][:, :], ALU.mult)\
                    .then_inc(ln[k]["shift"], 1)

            def adj_add(n):
                pool.wait_ge(s["adj_loaded"], n * 16 + 16)
                after(pool, "agg0_ps", n)
                nc.gpsimd.tensor_tensor(adj_eye[:, :, :], adj_in[:, :, :], eye_eps[:, :, :], ALU.add)\
                    .then_inc(s["adj_done"], 1)

            def x_b2_add(n):
                pool.wait_ge(s["x_loaded"], n * 16 + 16)
                after(pool, "x1_new_done", n)
                nc.gpsimd.tensor_tensor(x_b2[:, :, :], x_in[:, :, :], wide(g0_b2[:, :], 1, G), ALU.add)\
                    .then_inc(s["x_b2_done"], 1)

            def x3_tokens_add(n):
                pool.wait_ge(ln[3]["normed"], n * G + G)
                after(pool, "out_done", n)
                nc.gpsimd.tensor_tensor(x3_tokens[:, :, :], x3[:, :, :], normed[3][:, :, :], ALU.add)\
                    .then_inc(s["x3_tokens_done"], 1)

            def start():
                nc.gpsimd.memset(pow_half[:, :], -0.5).then_inc(s["pool_consts"], 1)
                nc.gpsimd.memset(pow_base[:, :], 2.718281828459045).then_inc(s["pool_consts"], 1)
                nc.gpsimd.memset(supp_t[:, :, :], 0.0).then_inc(s["consts_set"], 1)
                for k in range(2):
                    nc.gpsimd.memset(rows[k][:, :, :], 0.0).then_inc(s["consts_set"], 1)
                pool.wait_ge(s["consts_set"], 3)
                nc.gpsimd.memset(rows[0][:, :, ONES:ONES + E], 1.0).then_inc(s["consts_set"], 1)
                pool.wait_ge(s["pool_consts"], 2)
                rstd_pow(0, 0)
                pool.wait_ge(s["small_loaded"], 16)
                pool.wait_ge(s["eye_eps_done"], 1)
                adj_add(0)
                x_b2_add(0)
                rstd_pow(1, 0)

            def early(i, c0, f0=True, q=True, pre=True, fin=True):
                n, m, r = i + 1, i + 3, early_ring(i)
                if fin:
                    hi1(c0 - 1, (r - 1) % RING, i * C1 + C1)
                for t in range(C0):
                    if f0:
                        hi0(c0 + t, (r + t) % RING)
                    if t == 1 and not q:
                        pool.wait_ge(s["fuse_d"], 1)
                        nc.gpsimd.tensor_tensor(fw[2][:, :], pow_base[:, 0:5], fw[1][:, :], ALU.pow)\
                            .then_inc(s["fuse_pow"], 1)
                    if t == 2 and pre:
                        adj_add(m)
                    if t == 3 and pre:
                        rstd_pow(0, m)
                    if t == 6 and pre:
                        x_b2_add(m)
                    if t == 8 and q:
                        rstd_pow(3, n)
                    if t == 10 and f0:
                        pool.wait_ge(s["deg_step"], (i + 2) * 3 + 3)
                        nc.gpsimd.tensor_tensor(raised[:, :], safe_degree[:, :], pow_half[:, 0:2], ALU.pow)\
                            .then_inc(s["deg_pow"], 1)
                    if t == 13 and pre:
                        rstd_pow(1, m)
                    if t == 15 and q:
                        x3_tokens_add(n)
                    if t == 12 and q:
                        pool.wait_ge(s["soft_d"], n + 1)
                        nc.gpsimd.tensor_tensor(power[:, :], pow_base[:, 0:G], exponent[:, :], ALU.pow)\
                            .then_inc(s["soft_e"], 1)

            def late(i, c0, f1=True, pre=True, back=True):
                r = late_ring(i)
                for t in range(C1):
                    if t == 5 and back:
                        rstd_pow(2, i + 1)
                    if f1 and t > 0:
                        hi1(c0 + t - 1, (r + t - 1) % RING, i * C1 + t)
                    if f1 and back and t - 1 in POOL_LO:
                        lo1(c0 + t - 1, (r + t - 1) % RING)

            def end(i, c):
                hi1(c - 1, (late_ring(i) + C1 - 1) % RING, i * C1 + C1)

            schedule(pool, late, early, start, end)

        @block_ctx.vector
        def _(dve):
            V = nc.vector

            def held():
                dve.sem_inc(s["dve_held"], 1)

            def lo(c, ring):
                dve.wait_ge(s["hi_done"], c + 1)
                V.tensor_tensor(h_lo[:, ring, :], hid[:, ring, :], h_hi[:, ring, :].bitcast(F32), ALU.subtract)\
                    .then_inc(s["lo_done"], 1)

            def weigh(c, ring, t, n):
                dve.wait_ge(s["gelu_done"], c + 1)
                dve.wait_ge(s["spread_ready"], n * C1 + t + 1)
                V.tensor_tensor(hid[:, ring, :], hid[:, ring, :], spread_bank(t)[:, :], ALU.mult)\
                    .then_inc(s["weighted_done"], 1)

            def norm_stats(k, n, src):
                for b in range(G):
                    V.bn_stats(stats[k][:, b, :], src[:, b, :]).then_inc(ln[k]["stats"], 1)
                dve.wait_ge(ln[k]["stats"], n * G + G)
                held()
                for b in range(G):
                    V.bn_aggr(mean_var[k][:, b, :], stats[k][:, b, :]).then_inc(ln[k]["moments"], 1)
                dve.wait_ge(ln[k]["moments"], n * G + G)
                V.tensor_scalar(var_eps[k][:, :], mean_var[k][:, :, 1], EPS, None, ALU.add).then_inc(ln[k]["var"], 1)
                V.tensor_scalar(minus_mean[k][:, :], mean_var[k][:, :, 0], -1.0, None, ALU.mult)\
                    .then_inc(ln[k]["minus"], 1)

            def xt_rest(k, n, ps):
                dve.wait_ge(s[f"xt_hi{k}"], n + 1)
                V.tensor_tensor(xt_lo[k][:, :], ps[:, :], xt_hi[k][:, :].bitcast(F32), ALU.subtract)\
                    .then_inc(s[f"xt_lo{k}"], 1)

            def rank_scores(k, n):
                link = chain(dve, f"pick_step{k}", n * (2 * G + 4))
                held()
                for b in range(G):
                    link(V.max(sorted_scores[k][:, b, :], score[k][:, b, :]), wait=(b == G - 1))
                if k:
                    V.tensor_tensor(exponent[:, :], sorted_scores[1][:, :, 1], sorted_scores[1][:, :, 0],
                                    ALU.subtract).then_inc(s["soft_d"], 1)
                second_best = sorted_scores[k][:, :, 1:2].to_broadcast([P, G, E])
                link(V.tensor_tensor(reaches[k][:, :, :], score[k][:, :, :], second_best, ALU.is_ge), wait=False)
                link(V.tensor_tensor(exceeds[k][:, :, :], score[k][:, :, :], second_best, ALU.is_gt))
                link(V.tensor_tensor(ranked[k][:, :, :], reaches[k][:, :, :], wide(rank[:, :], 1, G), ALU.mult))
                link(V.scalar_tensor_tensor(out=order[k][:, :, :], in0=exceeds[k][:, :, :], scalar=2.0 * E,
                                            in1=ranked[k][:, :, :], op0=ALU.mult, op1=ALU.add))

            def order_scores(k, n):
                link = chain(dve, f"pick_step{k}", n * (2 * G + 4) + G + 4)
                held()
                for b in range(G):
                    link(V.max(sorted_order[k][:, b, :], order[k][:, b, :]), wait=(b == G - 1))

            def gate_score(n):
                dve.wait_ge(s["score_ps0"], n + 1)
                parts = pb[:, 0:2 * G * E].rearrange("p (b a e) -> p b a e", b=G, a=2)
                V.tensor_tensor(score_b[:, :, :], parts[:, :, 0, :], wide(gate_b[:, :], 1, G), ALU.add)\
                    .then_inc(s["score_b_done"], 1)
                dve.wait_ge(s["score_b_done"], n + 1)
                V.tensor_tensor(score[0][:, :, :], parts[:, :, 1, :], score_b[:, :, :], ALU.add)\
                    .then_inc(s["score_done0"], 1)
                dve.wait_ge(s["score_done0"], n + 1)

            def gate_rows(n):
                order_scores(0, n)
                after(dve, "rows_ps0", n)
                V.tensor_tensor(rows[0][:, :, 0:ONES].rearrange("p b (k e) -> p b k e", k=PARTS),
                                wide(order[0][:, :, :], 2, PARTS),
                                sorted_order[0][:, :, 1:2].unsqueeze(2).to_broadcast([P, G, PARTS, E]), ALU.is_ge)\
                    .then_inc(s["rows_done0"], 1)

            def router_score(n):
                dve.wait_ge(s["score_ps1"], n + 1)
                parts = pb[:, 0:2 * G * E].rearrange("p (b a e) -> p b e a", b=G, a=2)
                V.tensor_reduce(score[1][:, :, :], parts, AX, ALU.add)\
                    .then_inc(s["score_done1"], 1)
                dve.wait_ge(s["score_done1"], n + 1)

            def router_chosen(n):
                order_scores(1, n)
                for place, dst in ((1, chosen), (0, first)):
                    V.tensor_tensor(dst[:, :, :], order[1][:, :, :],
                                    sorted_order[1][:, :, place:place + 1].to_broadcast([P, G, E]), ALU.is_ge)\
                        .then_inc(s["chosen_done"], 1)

            def router_rows(n):
                dve.wait_ge(s["soft_e"], n + 1)
                dve.wait_ge(s["chosen_done"], n * 2 + 2)
                link = chain(dve, "soft_step", n * 9)
                link(V.tensor_tensor(second[:, :, :], chosen[:, :, :], wide(power[:, :], 2, E), ALU.mult), wait=False)
                link(V.tensor_scalar(total[:, :], power[:, :], 1.0, 1e-12, ALU.add, ALU.max))
                link(V.tensor_tensor(picked[:, :, :], second[:, :, :], first[:, :, :], ALU.max), wait=False)
                link(V.reciprocal(per_total[:, :], total[:, :]))
                link(V.tensor_tensor(weight[:, :, :], picked[:, :, :], wide(per_total[:, :], 2, E), ALU.mult))
                after(dve, "rows_ps1", n)
                link(V.tensor_copy(rows[1][:, :, 0:E], weight[:, :, :]))
                link(V.tensor_tensor(weight_rest[:, :, :], weight[:, :, :], rows[1][:, :, 0:E], ALU.subtract))
                link(V.tensor_copy(rows[1][:, :, E:2 * E], weight_rest[:, :, :]))
                link(V.tensor_tensor(weight_rest2[:, :, :], weight_rest[:, :, :], rows[1][:, :, E:2 * E],
                                     ALU.subtract))
                V.tensor_copy(rows[1][:, :, 2 * E:3 * E], weight_rest2[:, :, :]).then_inc(s["rows_done1"], 1)

            def x1_add(n):
                dve.wait_ge(s["x1_ps"], n + 1)
                dve.wait_ge(s["x_b2_done"], n + 1)
                after(dve, "x1_done", n)
                V.tensor_tensor(x1_new[:, :, :].rearrange("p b d -> p (b d)"), pa[:, :],
                                x_b2[:, :, :].rearrange("p b d -> p (b d)"), ALU.add).then_inc(s["x1_new_done"], 1)

            def x2_add(n):
                dve.wait_ge(s["y0_back"], n + 1)
                dve.wait_ge(s["x1_done"], n + 1)
                V.tensor_tensor(x2[:, :, :].rearrange("p b d -> p (b d)"), pa[:, :],
                                x1[:, :, :].rearrange("p b d -> p (b d)"), ALU.add).then_inc(s["x2_done"], 1)

            def x3_add(n):
                dve.wait_ge(s["fuse_ps"], n + 1)
                after(dve, "x3_tokens_done", n)
                V.tensor_tensor(x3[:, :, :].rearrange("p b d -> p (b d)"), pb[:, :],
                                x2[:, :, :].rearrange("p b d -> p (b d)"), ALU.add).then_inc(s["x3_done"], 1)

            def out_add(n):
                dve.wait_ge(s["y1_back"], n + 1)
                dve.wait_ge(s["x3_tokens_done"], n + 1)
                after(dve, "out_stored", n * 16)
                V.tensor_tensor(x_out[:, :, :].rearrange("p b d -> p (b d)"), pa[:, :],
                                x3_tokens[:, :, :].rearrange("p b d -> p (b d)"), ALU.add).then_inc(s["out_done"], 1)

            def block_prepare(n):
                dve.wait_ge(s["block_loaded"], n * 16 + 16)
                V.tensor_tensor(block[:, :, :], block_in[:, :, :], wide(ident[:, :], 1, 2), ALU.add)\
                    .then_inc(s["block_eye"], 1)
                dve.wait_ge(s["block_eye"], n + 1)
                link = chain(dve, "deg_step", n * 3)
                link(V.tensor_reduce(degree[:, :], block[:, :, :], AX, ALU.add))
                link(V.tensor_scalar(no_degree[:, :], degree[:, :], 0.0, None, ALU.is_equal))
                V.tensor_tensor(safe_degree[:, :], degree[:, :], no_degree[:, :], ALU.add).then_inc(s["deg_step"], 1)

            def block_scale(n):
                dve.wait_ge(s["deg_pow"], n + 1)
                V.scalar_tensor_tensor(out=has_degree[:, :], in0=no_degree[:, :], scalar=-1.0, in1=raised[:, :],
                                       op0=ALU.mult, op1=ALU.mult).then_inc(s["dinv_done"], 1)
                dve.wait_ge(s["dinv_done"], n * 2 + 1)
                V.tensor_tensor(dinv[:, :], raised[:, :], has_degree[:, :], ALU.add).then_inc(s["dinv_done"], 1)
                dve.wait_ge(s["dinv_done"], n * 2 + 2)
                after(dve, "norm_ps", n)
                V.tensor_tensor(block_row[:, :, :], block[:, :, :], wide(dinv[:, :], 2, P), ALU.mult)\
                    .then_inc(s["block_row_done"], 1)

            def norm_evacuate(n):
                dve.wait_ge(s["norm_ps"], n + 1)
                after(dve, "conv_ps", n)
                V.tensor_tensor(norm_t[:, :, :], pa[:, 0:2 * P].rearrange("p (a n) -> p a n", a=2),
                                wide(dinv[:, :], 2, P), ALU.mult).then_inc(s["norm_t_done"], 1)

            def hid1_bias(n):
                dve.wait_ge(s["hid1_ps"], n + 1)
                after(dve, "hid1_done", n)
                for c in range(2):
                    V.tensor_tensor(hid1_b[:, c, :, 0:USED],
                                    pb[:, c * G * S:(c + 1) * G * S].rearrange("p (b n) -> p b n", b=G)[:, :, 0:USED],
                                    wide(g1_b1[:, c, 0:USED], 1, G), ALU.add).then_inc(s["hid1_b_done"], 1)

            def conv_bias(n):
                dve.wait_ge(s["conv_ps"], n + 1)
                after(dve, "conv_done", n)
                V.tensor_tensor(conv_b[:, :, :], pb[:, 0:2 * P].rearrange("p (a d) -> p a d", a=2),
                                wide(g1_b2[:, :], 1, 2), ALU.add).then_inc(s["conv_b_done"], 1)

            def split_lo(k):
                dve.wait_ge(s["w_hi_done"], k + 1)
                V.tensor_tensor(w_lo[:, k, :], stage[:, k % 2, :], w_hi[:, k, :].bitcast(F32), ALU.subtract)\
                    .then_inc(s["w_lo_done"], 1)

            def split_b2():
                link = chain(dve, "b2_step", 0)
                link(V.tensor_copy(b2_part[:, 0, :, :], e_b2[:, :, :]))
                link(V.tensor_tensor(b2_rest[:, :, :], e_b2[:, :, :], b2_part[:, 0, :, :], ALU.subtract))
                link(V.tensor_copy(b2_part[:, 1, :, :], b2_rest[:, :, :]))
                link(V.tensor_tensor(b2_rest2[:, :, :], b2_rest[:, :, :], b2_part[:, 1, :, :], ALU.subtract))
                link(V.tensor_copy(b2_part[:, 2, :, :], b2_rest2[:, :, :]))
                link(V.tensor_scalar(b2_mix[:, 0, :], b2_part[:, 0, 0, :], part_rows[:, 0:1], None, ALU.mult))
                link(V.scalar_tensor_tensor(out=b2_mix[:, 1, :], in0=b2_part[:, 1, 0, :], scalar=part_rows[:, 1:2],
                                            in1=b2_mix[:, 0, :], op0=ALU.mult, op1=ALU.add))
                V.scalar_tensor_tensor(out=e0_b2[:, :], in0=b2_part[:, 2, 0, :], scalar=part_rows[:, 2:3],
                                       in1=b2_mix[:, 1, :], op0=ALU.mult, op1=ALU.add).then_inc(s["e0_b2_done"], 1)

            def fuse_start():
                dve.wait_ge(s["late_loaded"], 16)
                link = chain(dve, "fuse_step", 0)
                link(V.tensor_reduce(fw_col[0][:, :], fuse_w[:, :], AX, ALU.max))
                V.tensor_scalar(fw[1][:, :], fuse_w[:, :], fw_col[0][:, 0:1], None, ALU.subtract)\
                    .then_inc(s["fuse_d"], 1)

            def fuse_finish():
                dve.wait_ge(s["fuse_pow"], 1)
                link = chain(dve, "fuse_step", 1)
                link(V.tensor_reduce(fw_col[1][:, :], fw[2][:, :], AX, ALU.add))
                link(V.reciprocal(fw_col[2][:, :], fw_col[1][:, :]))
                link(V.scalar_tensor_tensor(out=fw[3][:, :], in0=fw[2][:, :], scalar=fw_col[2][:, 0:1],
                                            in1=slot_group[:, :], op0=ALU.mult, op1=ALU.mult))
                link(V.tensor_reduce(fw_col[3][:, :], fw[3][:, :], AX, ALU.add))
                V.tensor_scalar(fuse[:, :, :], slot_token[:, :, :], fw_col[3][:, 0:1], None, ALU.mult)\
                    .then_inc(s["fuse_done"], 1)

            def start():
                dve.wait_ge(s["x_loaded"], 16)
                norm_stats(0, 0, x_in)
                dve.wait_ge(s["small_loaded"], 16)
                V.tensor_scalar(eps_col[:, :], eps_in[:, :], 1.0, None, ALU.add).then_inc(s["eps_done"], 1)
                dve.wait_ge(s["eps_done"], 1)
                V.tensor_scalar(eye_eps[:, :, :], wide(ident[:, :], 1, G), eps_col[:, 0:1], None, ALU.mult)\
                    .then_inc(s["eye_eps_done"], 1)
                dve.wait_ge(s["gate_w_hi"], 1)
                V.tensor_tensor(gate_part[:, :, 1, :], gate_w[:, :, :], gate_part[:, :, 0, :].bitcast(F32), ALU.subtract)\
                    .then_inc(s["gate_w_lo"], 1)
                split_b2()
                split_lo(0)
                x1_add(0)
                dve.wait_ge(s["x1_new_done"], 1)
                norm_stats(1, 0, x1_new)
                xt_rest(0, 0, pa)
                gate_score(0)
                rank_scores(0, 0)
                dve.wait_ge(s["consts_set"], 4)
                gate_rows(0)
                split_lo(1)

            def early(i, c0, f0=True, q=True, pre=True, fin=True):
                n, m, r = i + 1, i + 3, early_ring(i)
                if fin:
                    weigh(c0 - 1, (r - 1) % RING, C1 - 1, i)
                    lo(c0 - 2, (r - 2) % RING)
                for t in range(C0):
                    if t == 1 and fin:
                        lo(c0 - 1, (r - 1) % RING)
                    if t > 0 and f0:
                        lo(c0 + t - 1, (r + t - 1) % RING)
                    if t == 0 and not q:
                        fuse_start()
                    if t == 5 and not q:
                        split_lo(2)
                        fuse_finish()
                    if t == 2 and q:
                        hid1_bias(n)
                    if t == 1 and pre:
                        dve.wait_ge(s["x_loaded"], m * 16 + 16)
                        norm_stats(0, m, x_in)
                    if t == 6 and q:
                        conv_bias(n)
                    if t == 5 and fin:
                        out_add(i)
                    if t == 7 and q:
                        x3_add(n)
                        dve.wait_ge(s["x3_done"], n + 1)
                        norm_stats(3, n, x3)
                    if t == 9 and f0:
                        block_prepare(i + 2)
                    if t == 10 and q:
                        xt_rest(1, n, pb)
                    if t == 11 and f0:
                        block_scale(i + 2)
                    if t == 12 and q:
                        router_score(n)
                        rank_scores(1, n)
                    if t == 12 and pre:
                        x1_add(m)
                    if t == 13 and q:
                        router_chosen(n)
                    if t == 13 and pre:
                        dve.wait_ge(s["x1_new_done"], m + 1)
                        norm_stats(1, m, x1_new)
                    if t == 14 and q:
                        router_rows(n)

            def late(i, c0, f1=True, pre=True, back=True):
                r = late_ring(i)
                for t in range(C1):
                    if t == 0 and back:
                        lo(c0 - 1, (r - 1) % RING)
                    ahead = f1 and t > 0 and not back
                    if ahead:
                        weigh(c0 + t - 1, (r + t - 1) % RING, t - 1, i)
                    if f1 and t > 1 and not (back and t - 2 in POOL_LO):
                        lo(c0 + t - 2, (r + t - 2) % RING)
                    if f1 and t > 0 and not ahead:
                        weigh(c0 + t - 1, (r + t - 1) % RING, t - 1, i)
                    if t == 0 and back:
                        norm_evacuate(i + 1)
                    if t == 1 and pre:
                        xt_rest(0, i + 2, pa)
                    if t == 2 and pre:
                        gate_score(i + 2)
                        rank_scores(0, i + 2)
                    if t == 3 and pre:
                        gate_rows(i + 2)
                    if t == 4 and back:
                        x2_add(i + 1)
                        dve.wait_ge(s["x2_done"], i + 2)
                        norm_stats(2, i + 1, x2)

            def end(i, c):
                r = late_ring(i)
                weigh(c - 1, (r + C1 - 1) % RING, C1 - 1, i)
                lo(c - 2, (r + C1 - 2) % RING)
                lo(c - 1, (r + C1 - 1) % RING)
                out_add(i)

            schedule(dve, late, early, start, end)

        @block_ctx.tensor
        def _(pe):
            mm = nc.tensor.matmul

            def three(dst, w_hi_, w_lo_, x_hi_, x_lo_, first_=True, last_=True):
                mm(dst, w_hi_, x_hi_, start=first_, stop=False)
                mm(dst, w_hi_, x_lo_, start=False, stop=False)
                return mm(dst, w_lo_, x_hi_, start=False, stop=last_)

            def expert_w(part, third, at):
                return part[:, third, at * P:(at + 1) * P]

            def z0(c, ring, t, n):
                if t == 0:
                    pe.wait_ge(s["xt_lo0"], n + 1)
                after(pe, "gelu_done", c - Z_RING + 1)
                three(z[ring % Z_RING][:, :], expert_w(w_hi, 0, t), expert_w(w_lo, 0, t), xt_hi[0][:, :], xt_lo[0][:, :],
                      last_=False)
                if t == 0:
                    pe.wait_ge(s["rows_t0"], n + 1)
                mm(z[ring % Z_RING][:, :], shut[:, t // 2, :], rows_t[0][:, :], start=False, stop=True)\
                    .then_inc(s["z_ready"], 1)

            def y_0(c, ring, t, n):
                if t == 0:
                    after(pe, "y0_t", n)
                    after(pe, "weighted_done", n * C1 - C1)
                pe.wait_ge(s["lo_done"], c + 1)
                if t == C0 - 1:
                    mm(y0[:, :], e0_b2[:, :], rows_t[0][:, :], start=False, stop=False)
                last = three(y0[:, :], expert_w(w_hi, 1, t), expert_w(w_lo, 1, t), h_hi[:, ring, :], h_lo[:, ring, :],
                             first_=(t == 0), last_=(t == C0 - 1))
                last.then_inc(s["y_done"], 1)

            def z1(c, ring, t, n):
                if t == 0:
                    pe.wait_ge(s["xt_lo1"], n + 1)
                after(pe, "gelu_done", c - Z_RING + 1)
                three(z[ring % Z_RING][:, :], expert_w(w_hi, 2, t), expert_w(w_lo, 2, t), xt_hi[1][:, :], xt_lo[1][:, :])\
                    .then_inc(s["z_ready"], 1)

            def spread1(t, n):
                if t == 0:
                    pe.wait_ge(s["rows_t1"], n + 1)
                    after(pe, "weighted_done", n * C1)
                elif t == 1:
                    after(pe, "y1_t", n)
                elif t == 3:
                    more = 1 if isinstance(n, int) and n == GROUPS - 1 else 2
                    pe.wait_ge(s["y0_t"], n + more)
                else:
                    pe.wait_ge(s["weighted_done"], n * C1 + t - 1)
                mm(spread_bank(t)[:, :], pick[:, t, :], rows_t[1][:, :], start=True, stop=True).then_inc(s["spread_ready"], 1)

            def y_1(c, ring, t, n):
                if t == 0:
                    pe.wait_ge(s["weighted_done"], n * C1 + 2)
                pe.wait_ge(s["lo_done"], c + 1)
                if t == C1 - 1:
                    for k in range(PARTS):
                        mm(y1[:, :], b2_part[:, k, 1, :], rows_t[1][:, :], start=False, stop=False)
                last = three(y1[:, :], expert_w(w_hi, 2, C1 + t), expert_w(w_lo, 2, C1 + t), h_hi[:, ring, :],
                             h_lo[:, ring, :], first_=(t == 0), last_=(t == C1 - 1))
                last.then_inc(s["y_done"], 1)

            def turn4(ps, src, name):
                for b in range(G):
                    last = nc.tensor.transpose(ps[:, b * P:(b + 1) * P], src(b), ident[:, :])
                last.then_inc(s[name], 1)

            def agg0_mm(n):
                pe.wait_ge(ln[0]["normed"], n * G + G)
                pe.wait_ge(s["adj_done"], n + 1)
                for b in range(G):
                    last = mm(pa[:, b * P:(b + 1) * P], normed[0][:, b, :], adj_eye[:, b, :], start=True, stop=True)
                last.then_inc(s["agg0_ps"], 1)

            def hid0_mm(n, c):
                if c == 0:
                    pe.wait_ge(s["agg0_done"], n + 1)
                else:
                    pe.wait_ge(s["hid0_done"], n * 2 + 1)
                mm(pa[:, :], g0_w1[:, c * P:(c + 1) * P], agg0[:, :], start=True, stop=True).then_inc(s["hid0_ps"], 1)

            def x1_mm(n):
                pe.wait_ge(s["hid0_done"], n * 2 + 2)
                for b in range(G):
                    for c in range(2):
                        last = mm(pa[:, b * P:(b + 1) * P], hid0[:, c, b * P:(b + 1) * P], g0_w2[:, c, :],
                                  start=(c == 0), stop=(c == 1))
                last.then_inc(s["x1_ps"], 1)

            def xt_mm(k, n, ps):
                pe.wait_ge(ln[3 if k else 1]["normed"], n * G + G)
                turn4(ps, lambda b: normed[3 if k else 1][:, b, :], f"xt_ps{k}")

            def score_mm(k, n, ps):
                pe.wait_ge(s[f"xt_lo{k}"], n + 1)
                for b in range(G):
                    dst, at = ps[:, b * 2 * E:(b + 1) * 2 * E], slice(b * P, (b + 1) * P)
                    mm(dst, xt_hi[k][:, at], gate_part[:, k, :, :].rearrange("d a e -> d (a e)"), start=True, stop=False)
                    last = mm(dst[:, 0:E], xt_lo[k][:, at], gate_part[:, k, 0, :], start=False, stop=True)
                last.then_inc(s[f"score_ps{k}"], 1)

            def rows_mm(k, n):
                pe.wait_ge(s[f"rows_done{k}"], n + 1)
                for b in range(G):
                    last = nc.tensor.transpose(pb[:, :].bitcast(BF16)[:, b * P:(b + 1) * P], rows[k][:, b, :],
                                               identb[:, :])
                last.then_inc(s[f"rows_ps{k}"], 1)

            def y_back(k, n):
                pe.wait_ge(s[f"y{k}_t"], n + 1)
                src = y1_t if k else y0_t
                turn4(pa, lambda b: src[:, b * P:(b + 1) * P], f"y{k}_back")

            def norm_mm(n):
                pe.wait_ge(s["block_row_done"], n + 1)
                for p in range(2):
                    last = nc.tensor.transpose(pa[:, p * P:(p + 1) * P], block_row[:, p, :], ident[:, :])
                last.then_inc(s["norm_ps"], 1)

            def tok_mm(n):
                pe.wait_ge(s["norm_t_done"], n + 1)
                for p in range(2):
                    last = mm(pb[:, p * P:(p + 1) * P].rearrange("t (a n) -> t a n", a=2), slot_token[:, p, :],
                              norm_t[:, :, p * S:(p + 1) * S], start=True, stop=True)
                last.then_inc(s["tok_ps"], 1)

            def agg1_mm(n):
                pe.wait_ge(ln[2]["normed"], n * G + G)
                pe.wait_ge(s["norm_tok_done"], n + 1)
                for b in range(G):
                    last = mm(pa[:, b * S:(b + 1) * S], normed[2][:, b, :], norm_tok[:, b % 2, b // 2, :],
                              start=True, stop=True)
                last.then_inc(s["agg1_ps"], 1)

            def hid1_mm(n):
                pe.wait_ge(s["agg1_done"], n + 1)
                for c in range(2):
                    ps = pb[:, c * G * S:(c + 1) * G * S].rearrange("p (b n) -> p b n", b=G)
                    for g, nodes in enumerate(NODES):
                        at = slice(FIRST[g], FIRST[g] + len(nodes))
                        last = mm(ps[:, :, at], g1_w1[:, g, c, :], agg1[:, :, at], start=True, stop=True)
                last.then_inc(s["hid1_ps"], 1)

            def supp_t_mm(n):
                pe.wait_ge(s["hid1_done"], n + 1)
                ps = pb[:, 0:G * S].rearrange("p (b n) -> p b n", b=G)
                for g, nodes in enumerate(NODES):
                    at = slice(FIRST[g], FIRST[g] + len(nodes))
                    for c in range(2):
                        last = mm(ps[:, :, at], g1_w2[:, g, c, :], hid1[:, c, :, at], start=(c == 0), stop=(c == 1))
                last.then_inc(s["supp_t_ps"], 1)

            def supp_mm(n):
                pe.wait_ge(s["supp_t_done"], n + 1)
                for p in range(2):
                    last = nc.tensor.transpose(pb[:, p * P:(p + 1) * P],
                                               supp_t[:, 2 * p:2 * p + 2, :].rearrange("d b n -> d (b n)"),
                                               ident[:, :])
                last.then_inc(s["supp_ps"], 1)

            def conv_mm(n):
                pe.wait_ge(s["supp_done"], n + 1)
                for p in range(2):
                    last = mm(pb[:, p * P:(p + 1) * P], norm_t[:, p, :], supp[:, p, :], start=True, stop=True)
                last.then_inc(s["conv_ps"], 1)

            def fuse_mm(n):
                pe.wait_ge(s["conv_done"], n + 1)
                for b in range(G):
                    last = mm(pb[:, b * P:(b + 1) * P], fuse[:, b % 2, :], conv[:, b // 2, :], start=True, stop=True)
                last.then_inc(s["fuse_ps"], 1)

            def start():
                pe.wait_ge(s["small_loaded"], 16)
                agg0_mm(0)
                hid0_mm(0, 0)
                hid0_mm(0, 1)
                x1_mm(0)
                xt_mm(0, 0, pa)
                pe.wait_ge(s["gate_w_lo"], 1)
                score_mm(0, 0, pb)
                pe.wait_ge(s["bf16_consts"], 3)
                rows_mm(0, 0)
                pe.wait_ge(s["w_lo_done"], 1)
                pe.wait_ge(s["e0_b2_done"], 1)

            def early(i, c0, f0=True, q=True, pre=True, fin=True):
                n, m, r = i + 1, i + 3, early_ring(i)
                for t in range(C0):
                    if f0:
                        z0(c0 + t, (r + t) % RING, t, i + 2)
                    if t == 1 and q:
                        pe.wait_ge(s["x2_done"], n + 1)
                        agg1_mm(n)
                    if t == 2 and q:
                        if f0:
                            pe.wait_ge(s["rows_t0"], i + 3)
                        else:
                            pe.wait_ge(s["norm_tok_done"], n + 1)
                        if not fin:
                            pe.wait_ge(s["late_loaded"], 16)
                        hid1_mm(n)
                    if t == 4 and q:
                        pe.wait_ge(s["hid1_b_done"], n * 2 + 2)
                        supp_t_mm(n)
                    if t == 5 and q:
                        supp_mm(n)
                    if t == 6 and q:
                        conv_mm(n)
                    if t < LAG and fin:
                        y_1(c0 + t - LAG, (r + t - LAG) % RING, C1 + t - LAG, i)
                    if t == LAG and not q:
                        pe.wait_ge(s["w_lo_done"], 2)
                    if t >= LAG and f0:
                        y_0(c0 + t - LAG, (r + t - LAG) % RING, t - LAG, i + 2)
                    if t == 0 and fin:
                        spread1(C1 - 1, i)
                    if t == LAG and fin:
                        if q:
                            pe.wait_ge(s["agg1_done"], n + 1)
                        y_back(1, i)
                    if t == 7 and pre:
                        after(pe, "out_done", i + 1)
                        if not q:
                            pe.wait_ge(s["xt_lo0"], 1)
                        agg0_mm(m)
                    if t == 7 and q:
                        pe.wait_ge(s["conv_b_done"], n + 1)
                        if not fin:
                            pe.wait_ge(s["fuse_done"], 1)
                        fuse_mm(n)
                    if t == 8 and pre:
                        hid0_mm(m, 0)
                    if t == 10 and pre:
                        hid0_mm(m, 1)
                    if t == 10 and q:
                        pe.wait_ge(s["x3_done"], n + 1)
                        xt_mm(1, n, pb)
                    if t == 11 and q:
                        score_mm(1, n, pb)
                    if t == 11 and pre:
                        x1_mm(m)
                if q and not fin:
                    pe.wait_ge(s["w_lo_done"], 3)

            def late(i, c0, f1=True, pre=True, back=True):
                r = late_ring(i)
                for t in range(C1):
                    if f1:
                        z1(c0 + t, (r + t) % RING, t, i)
                    if t == 1 and f1:
                        pe.wait_ge(s["score_done1"], i + 1)
                        rows_mm(1, i)
                    if t < LAG and back:
                        y_0(c0 + t - LAG, (r + t - LAG) % RING, C0 + t - LAG, i + 1)
                    if t >= LAG and f1:
                        y_1(c0 + t - LAG, (r + t - LAG) % RING, t - LAG, i)
                    if t > 0 and f1:
                        spread1(t - 1, i)
                    if t == 5 and pre:
                        pe.wait_ge(s["score_done0"], i + 3)
                        rows_mm(0, i + 2)
                    if t == 0 and back:
                        if pre:
                            pe.wait_ge(s["x1_new_done"], i + 3)
                        else:
                            pe.wait_ge(s["out_done"], i)
                        norm_mm(i + 1)
                    if t == 1 and pre:
                        pe.wait_ge(s["norm_t_done"], i + 2)
                        xt_mm(0, i + 2, pa)
                    if t == 1 and back:
                        after(pe, "rows_t1", i + 1)
                        tok_mm(i + 1)
                    if t == 2 and pre:
                        pe.wait_ge(s["norm_tok_done"], i + 2)
                        score_mm(0, i + 2, pb)
                    if t == 4 and back:
                        if pre:
                            pe.wait_ge(s["xt_lo0"], i + 3)
                        else:
                            pe.wait_ge(s["norm_t_done"], i + 2)
                        y_back(0, i + 1)

            def end(i, c):
                r = late_ring(i)
                spread1(C1 - 1, i)
                for t in range(C1 - LAG, C1):
                    y_1(c - C1 + t, (r + t) % RING, t, i)
                y_back(1, i)

            schedule(pe, late, early, start, end)


def constants():
    import numpy as np

    ident = np.eye(P, dtype=np.float32)
    far = 2.0 ** 100
    shut = np.zeros((P, E), np.float32)
    pick = np.zeros((P, E), np.float32)
    for e in range(E):
        shut[e, e] = far
        shut[ONES, e] = -far
        for k in range(PARTS):
            pick[k * E + e, e] = 1
    part_rows = np.zeros((P, PARTS), np.float32)
    for k in range(PARTS):
        part_rows[k * E:(k + 1) * E, k] = 1
    slot_token = np.zeros((P, 2, P), np.float32)
    slot_group = np.zeros((P, 5), np.float32)
    for g, nodes in enumerate(NODES):
        for k, token in enumerate(nodes):
            for p in range(2):
                slot_token[p * S + FIRST[g] + k, p, token] = 1
                slot_group[p * S + FIRST[g] + k, g] = 1
    return {"ident": ident,
            "rank": np.tile(np.arange(E, 0, -1, dtype=np.float32), (P, 1)),
            "shut_rows": shut, "pick_rows": pick,
            "part_rows": part_rows, "slot_token": slot_token, "slot_group": slot_group}


def layout(v):
    import numpy as np

    def rows(name):
        return np.broadcast_to(v[name].reshape(1, -1), (P, v[name].size))

    adj = v["adj"]
    block = np.zeros((P, PAIRS, P), adj.dtype)
    slot_b1 = np.zeros((P, 2, S), adj.dtype)
    slot_b2 = np.zeros((P, P), adj.dtype)
    for g, nodes in enumerate(NODES):
        for k, token in enumerate(nodes):
            slot_b1[:, :, FIRST[g] + k] = v["L1_gnn_b1"][g].reshape(2, P).T
            for p in range(2):
                slot = p * S + FIRST[g]
                block[slot + k, :, slot:slot + len(nodes)] = adj[p::2, token][:, nodes]
                slot_b2[slot + k] = v["L1_gnn_b2"][g]
    e_b2 = np.zeros((P, 2, P), adj.dtype)
    for k in range(PARTS):
        e_b2[k * E:(k + 1) * E, 0] = v["L0_ffn_b2"]
        e_b2[k * E:(k + 1) * E, 1] = v["L1_ffn_b2"]
    w1 = v["L1_ffn_w1"].transpose(1, 0, 2).reshape(P, E * P)
    w2 = v["L1_ffn_w2"].transpose(1, 0, 2).reshape(P, E * P)
    return {
        "x": v["x"].transpose(1, 0, 2),
        "adj": adj.transpose(2, 0, 1),
        "block": block,
        "eps": rows("L0_gnn_eps"),
        "g0_w1": v["L0_gnn_W1"],
        "g0_w2": v["L0_gnn_W2"].reshape(2, P, P).transpose(1, 0, 2),
        "g0_b1": v["L0_gnn_b1"].reshape(2, P).T,
        "g0_b2": rows("L0_gnn_b2"),
        "gate_w": np.stack([v["L0_ffn_Wg"], v["L1_ffn_router_w"].T], axis=1),
        "gate_b": rows("L0_ffn_bg"),
        "e0_w1": v["L0_ffn_W1"].transpose(1, 0, 2).reshape(P, C0 * P),
        "e0_w2": v["L0_ffn_W2"].reshape(E, 2, P, P).transpose(2, 0, 1, 3).reshape(P, C0 * P),
        "e0_b1": v["L0_ffn_b1"].reshape(C0, P).T,
        "e1_w": np.concatenate([w1, w2], axis=1),
        "e1_b1": v["L1_ffn_b1"].T,
        "e_b2": e_b2,
        "g1_w1": v["L1_gnn_W1"].reshape(5, P, 2, P).transpose(1, 0, 2, 3),
        "g1_w2": v["L1_gnn_W2"].reshape(5, 2, P, P).transpose(2, 0, 1, 3),
        "g1_b1": slot_b1,
        "g1_b2": slot_b2,
        "fuse_w": rows("L1_gnn_fusion_w"),
    }


def kernel(**inputs):
    import concourse.bacc as bacc
    import numpy as np
    from concourse.bass_utils import run_bass_kernel_spmd

    nc = bacc.Bacc("TRN2", target_bir_lowering=False, num_devices=1)
    arrays, args = {}, {}
    values = {name: np.asarray(value) for name, value in inputs.items()}
    found = {**layout(values), **constants()}
    for together, fields in (("small", SMALL), ("late", LATE)):
        found[together] = np.concatenate([found.pop(name).reshape(P, size(shape)) for name, shape in fields.items()],
                                         axis=1)
    for name, value in found.items():
        value = np.ascontiguousarray(value)
        arrays[f"in_{name}"] = value
        args[name] = nc.dram_tensor(f"in_{name}", value.shape, mybir.dt.from_np(value.dtype),
                                    kind="ExternalInput").ap()
    out = nc.dram_tensor("out_x", (P, B, P), F32, kind="ExternalOutput").ap()
    program(nc, args, out)
    result = run_bass_kernel_spmd(nc, [arrays], core_ids=[0]).results[0]["out_x"]
    return np.ascontiguousarray(result.transpose(1, 0, 2))
```
